# Optimizing a Trainium2 kernel written in Bass

```python
import numpy as np
import jax
import jax.numpy as jnp

def _softmax(x, axis=-1):
    return jax.nn.softmax(x, axis=axis)

def _gelu(x):
    return jax.nn.gelu(x, approximate=True)

def _silu(x):
    return jax.nn.silu(x)

def _sigmoid(x):
    return jax.nn.sigmoid(x)

def _layernorm(x, axis=-1, eps=1e-05):
    m = jnp.mean(x, axis=axis, keepdims=True)
    v = jnp.var(x, axis=axis, keepdims=True)
    return (x - m) / jnp.sqrt(v + eps)

def _scatter_add(tgt, idx, src, axis=0):
    return tgt.at[idx].add(src)

def _segment_sum(src, seg, n):
    return jax.ops.segment_sum(src, seg, n)
kernel_name = 'mk_gnn_resnorm_d4_gnn_r8_c476ed'

def setup_inputs(seed: int=0):
    np.random.seed(seed)
    _w = jnp.asarray

    def _rec_inputs():
        import jax
        import jax.numpy as jnp
        _gk = jax.random.key(seed)
        x = -0.0005121 + 1.001 * jax.random.normal(jax.random.fold_in(_gk, 1), (6250, 64), jnp.float32)
        src = jax.random.randint(jax.random.fold_in(_gk, 2), (200000,), 0, 6250, jnp.int32)
        dst = jnp.minimum((6250 * jax.random.uniform(jax.random.fold_in(_gk, 3), (200000,)) ** 2.0).astype(jnp.int32), 49999)
        _o = jnp.argsort(dst, stable=True)
        src = src[_o]
        dst = dst[_o]
        edge_type_4 = jax.random.randint(jax.random.fold_in(_gk, 13), (200000,), 0, 4, jnp.int32)
        return (x, src, dst, edge_type_4)
    x, src, dst, edge_type_4 = _rec_inputs()

    def _L0_gnn_setup():
        import jax, jax.numpy as jnp
        import numpy as np
        N_NODES = 6250
        N_EDGES = 100000
        D_FEAT = 64
        key = jax.random.key(seed)
        k1, k2, k3 = jax.random.split(key, 3)
        xs = jax.random.normal(k1, (N_NODES, D_FEAT), dtype=jnp.float32)
        src = jax.random.randint(k2, (N_EDGES,), 0, N_NODES, dtype=jnp.int32)
        dst = jax.random.randint(k3, (N_EDGES,), 0, N_NODES, dtype=jnp.int32)
        return {'xs': xs, 'src': src, 'dst': dst}
    _L0_gnn_all = _L0_gnn_setup()
    _L0_gnn_in = {k: v for k, v in _L0_gnn_all.items() if k in ()}
    del _L0_gnn_all

    def _L1_gnn_setup():
        import jax, jax.numpy as jnp
        import numpy as np
        N, D, H, E = (6250, 64, 4, 100000)
        LN_EPS = 1e-05
        key = jax.random.key(seed)
        ks = jax.random.split(key, 8)
        x = jax.random.normal(ks[0], (N, D), dtype=jnp.float32)
        edge_index = jax.random.randint(ks[1], (2, E), 0, N, dtype=jnp.int64)
        lin_w = jax.random.normal(ks[2], (H * D, D), dtype=jnp.float32) * (1.0 / np.sqrt(D))
        bound = float(np.sqrt(6.0 / (H + D)))
        attn_src = jax.random.uniform(ks[3], (H, D), minval=-bound, maxval=bound, dtype=jnp.float32)
        attn_dst = jax.random.uniform(ks[4], (H, D), minval=-bound, maxval=bound, dtype=jnp.float32)
        out_w = jax.random.normal(ks[5], (D, H * D), dtype=jnp.float32) * (1.0 / np.sqrt(H * D))
        out_b = jnp.zeros((D,), dtype=jnp.float32)
        ln_g = jnp.ones((D,), dtype=jnp.float32)
        ln_b = jnp.zeros((D,), dtype=jnp.float32)
        return {'x': x, 'edge_index': edge_index, 'lin_w': lin_w, 'attn_src': attn_src, 'attn_dst': attn_dst, 'out_w': out_w, 'out_b': out_b, 'ln_g': ln_g, 'ln_b': ln_b}
    _L1_gnn_all = _L1_gnn_setup()
    _L1_gnn_in = {k: v for k, v in _L1_gnn_all.items() if k in ('lin_w', 'attn_src', 'attn_dst', 'out_w', 'out_b', 'ln_g', 'ln_b')}
    del _L1_gnn_all

    def _L2_gnn_setup():
        import jax, jax.numpy as jnp
        import numpy as np
        N_NODES = 6250
        N_EDGES = 100000
        IN_DIM = 64
        OUT_DIM = 64
        BN_EPS = 1e-05
        key = jax.random.key(seed)
        k1, k2, k3, k4 = jax.random.split(key, 4)
        feature = jax.random.normal(k1, (N_NODES, IN_DIM), dtype=jnp.float32)
        edge_index = jax.random.randint(k2, (2, N_EDGES), 0, N_NODES, dtype=jnp.int64)
        lim = 1.0 / np.sqrt(2 * IN_DIM)
        W = jax.random.uniform(k3, (OUT_DIM, 2 * IN_DIM), minval=-lim, maxval=lim, dtype=jnp.float32)
        b = jax.random.uniform(k4, (OUT_DIM,), minval=-lim, maxval=lim, dtype=jnp.float32)
        gamma = jnp.ones((OUT_DIM,), dtype=jnp.float32)
        beta = jnp.zeros((OUT_DIM,), dtype=jnp.float32)
        return {'feature': feature, 'edge_index': edge_index, 'W': W, 'b': b, 'gamma': gamma, 'beta': beta}
    _L2_gnn_all = _L2_gnn_setup()
    _L2_gnn_in = {k: v for k, v in _L2_gnn_all.items() if k in ('W', 'b', 'gamma', 'beta')}
    del _L2_gnn_all

    def _L3_gnn_setup():
        import jax, jax.numpy as jnp
        import numpy as np
        N = 6250
        E = 100000
        D = 64
        A = 64
        R = 4
        OUT = 64
        key = jax.random.key(seed)
        ks = jax.random.split(key, 10)
        h = jax.random.normal(ks[0], (N, D), jnp.float32)
        r = jax.random.normal(ks[1], (R, 2 * D, D), jnp.float32) * 0.1
        a = jax.random.normal(ks[2], (R, A), jnp.float32)
        Wa_w = jax.random.normal(ks[3], (A, 2 * D), jnp.float32) * (1.0 / np.sqrt(2 * D))
        Wa_b = jnp.zeros((A,), jnp.float32)
        lin_w = jax.random.normal(ks[4], (OUT, 2 * D), jnp.float32) * (1.0 / np.sqrt(2 * D))
        lin_b = jnp.zeros((OUT,), jnp.float32)
        src = jax.random.randint(ks[5], (E,), 0, N)
        dst = jax.random.randint(ks[6], (E,), 0, N)
        etype = jax.random.randint(ks[7], (E,), 0, R)
        return dict(h=h, r=r, a=a, Wa_w=Wa_w, Wa_b=Wa_b, lin_w=lin_w, lin_b=lin_b, src=src, dst=dst, etype=etype)
    _L3_gnn_all = _L3_gnn_setup()
    _L3_gnn_in = {k: v for k, v in _L3_gnn_all.items() if k in ('r', 'a', 'Wa_w', 'Wa_b', 'lin_w', 'lin_b')}
    del _L3_gnn_all
    return {'x': x, 'src': src, 'dst': dst, 'edge_type_4': edge_type_4, 'L1_gnn_lin_w': _L1_gnn_in['lin_w'], 'L1_gnn_attn_src': _L1_gnn_in['attn_src'], 'L1_gnn_attn_dst': _L1_gnn_in['attn_dst'], 'L1_gnn_out_w': _L1_gnn_in['out_w'], 'L1_gnn_out_b': _L1_gnn_in['out_b'], 'L1_gnn_ln_g': _L1_gnn_in['ln_g'], 'L1_gnn_ln_b': _L1_gnn_in['ln_b'], 'L2_gnn_W': _L2_gnn_in['W'], 'L2_gnn_b': _L2_gnn_in['b'], 'L2_gnn_gamma': _L2_gnn_in['gamma'], 'L2_gnn_beta': _L2_gnn_in['beta'], 'L3_gnn_r': _L3_gnn_in['r'], 'L3_gnn_a': _L3_gnn_in['a'], 'L3_gnn_Wa_w': _L3_gnn_in['Wa_w'], 'L3_gnn_Wa_b': _L3_gnn_in['Wa_b'], 'L3_gnn_lin_w': _L3_gnn_in['lin_w'], 'L3_gnn_lin_b': _L3_gnn_in['lin_b']}

def reference(x, src, dst, edge_type_4, L1_gnn_lin_w, L1_gnn_attn_src, L1_gnn_attn_dst, L1_gnn_out_w, L1_gnn_out_b, L1_gnn_ln_g, L1_gnn_ln_b, L2_gnn_W, L2_gnn_b, L2_gnn_gamma, L2_gnn_beta, L3_gnn_r, L3_gnn_a, L3_gnn_Wa_w, L3_gnn_Wa_b, L3_gnn_lin_w, L3_gnn_lin_b):
    import jax
    import jax.numpy as jnp

    def _L0_gnn_ref(xs, src, dst):
        import jax, jax.numpy as jnp
        import numpy as np
        N_NODES = 6250
        N_EDGES = 100000
        D_FEAT = 64
        gathered = xs[src]
        sums = jax.ops.segment_sum(gathered, dst, num_segments=N_NODES)
        counts = jax.ops.segment_sum(jnp.ones((src.shape[0],), dtype=xs.dtype), dst, num_segments=N_NODES)
        return sums / jnp.maximum(counts, 1.0)[:, None]

    def _L1_gnn_ref(x, edge_index, lin_w, attn_src, attn_dst, out_w, out_b, ln_g, ln_b):
        import jax, jax.numpy as jnp
        import numpy as np
        N, D, H, E = (6250, 64, 4, 100000)
        LN_EPS = 1e-05
        n, d = x.shape
        h = attn_src.shape[0]
        i, j = (edge_index[0], edge_index[1])
        xh = (x @ lin_w.T).reshape(n, h, d)
        a_dst = jnp.einsum('nhd,hd->nh', xh, attn_dst)
        a_src = jnp.einsum('nhd,hd->nh', xh, attn_src)
        alpha = a_dst[i] + a_src[j]
        alpha = jnp.where(alpha >= 0, alpha, 0.2 * alpha)
        ealpha = jnp.exp(alpha)
        denom = jax.ops.segment_sum(ealpha, i, num_segments=n)
        attn = ealpha / (denom[i] + 1e-09)
        out = jax.ops.segment_sum(attn[:, :, None] * xh[j], i, num_segments=n)
        out = out.reshape(n, h * d)
        out = out @ out_w.T + out_b
        out = jax.nn.elu(out) + x
        mu = jnp.mean(out, axis=-1, keepdims=True)
        var = jnp.var(out, axis=-1, keepdims=True)
        return (out - mu) / jnp.sqrt(var + LN_EPS) * ln_g + ln_b

    def _L2_gnn_ref(feature, edge_index, W, b, gamma, beta):
        import jax, jax.numpy as jnp
        import numpy as np
        N_NODES = 6250
        N_EDGES = 100000
        IN_DIM = 64
        OUT_DIM = 64
        BN_EPS = 1e-05
        src = edge_index[0]
        dst = edge_index[1]
        x_i = feature[dst]
        x_j = feature[src]
        m = jnp.concatenate([x_i, x_j - x_i], axis=-1)
        h = m @ W.T + b
        mu = jnp.mean(h, axis=0)
        var = jnp.var(h, axis=0)
        h = (h - mu) * jax.lax.rsqrt(var + BN_EPS) * gamma + beta
        h = jax.nn.relu(h)
        summed = jax.ops.segment_sum(h, dst, num_segments=N_NODES)
        deg = jax.ops.segment_sum(jnp.ones((h.shape[0],), h.dtype), dst, num_segments=N_NODES)
        return summed / jnp.maximum(deg, 1.0)[:, None]

    def _L3_gnn_ref(h, r, a, Wa_w, Wa_b, lin_w, lin_b, src, dst, etype):
        import jax, jax.numpy as jnp
        import numpy as np
        N = 6250
        E = 100000
        D = 64
        A = 64
        R = 4
        OUT = 64
        num_nodes = h.shape[0]
        hs = h[src]
        hd = h[dst]
        cat = jnp.concatenate([hd, hs], axis=-1)
        gate_logit = jnp.zeros((cat.shape[0], r.shape[-1]), cat.dtype)
        for i in range(r.shape[0]):
            gate_logit = gate_logit + jnp.where((etype == i)[:, None], cat @ r[i], 0.0)
        gate = jax.nn.sigmoid(gate_logit)
        att_feat = jax.nn.leaky_relu(cat @ Wa_w.T + Wa_b)
        a_sc = jnp.sum(att_feat * a[0], axis=-1)
        seg_max = jax.ops.segment_max(a_sc, dst, num_segments=num_nodes)
        ex = jnp.exp(a_sc - seg_max[dst])
        seg_sum = jax.ops.segment_sum(ex, dst, num_segments=num_nodes)
        att_n = ex / seg_sum[dst]
        scale = att_n[:, None] * gate
        msg = hs * scale
        h_N = jax.ops.segment_sum(msg, dst, num_segments=num_nodes)
        out = jnp.concatenate([h, h_N], axis=-1) @ lin_w.T + lin_b
        return jax.nn.leaky_relu(out)
    edge_index = jnp.stack([src, dst])
    x = _layernorm(x + _L0_gnn_ref(x, src, dst), axis=-1)
    x = _layernorm(x + _L1_gnn_ref(x, edge_index, L1_gnn_lin_w, L1_gnn_attn_src, L1_gnn_attn_dst, L1_gnn_out_w, L1_gnn_out_b, L1_gnn_ln_g, L1_gnn_ln_b), axis=-1)
    x = _layernorm(x + _L2_gnn_ref(x, edge_index, L2_gnn_W, L2_gnn_b, L2_gnn_gamma, L2_gnn_beta), axis=-1)
    x = _layernorm(x + _L3_gnn_ref(x, L3_gnn_r, L3_gnn_a, L3_gnn_Wa_w, L3_gnn_Wa_b, L3_gnn_lin_w, L3_gnn_lin_b, src, dst, edge_type_4), axis=-1)
    return x

_drawn_inputs = setup_inputs


def setup_inputs(seed=0):
    import zlib

    import numpy as np

    out = dict(_drawn_inputs(seed))
    spreads = {'L1_gnn_out_b': (0.0, 0.1),
     'L1_gnn_ln_g': (1.0, 0.2),
     'L1_gnn_ln_b': (0.0, 0.1),
     'L2_gnn_gamma': (1.0, 0.2),
     'L2_gnn_beta': (0.0, 0.1),
     'L3_gnn_Wa_b': (0.0, 0.395),
     'L3_gnn_lin_b': (0.0, 0.1)}
    factors = {'L2_gnn_b': 8.0}
    for name, (base, spread) in spreads.items():
        noise = np.random.default_rng([zlib.crc32(name.encode()), seed]).standard_normal(out[name].shape)
        drawn = base * np.exp(spread * noise) if base else spread * noise
        out[name] = jnp.asarray(drawn.astype(out[name].dtype))
    for name, factor in factors.items():
        out[name] = (out[name] * factor).astype(out[name].dtype)
    return out
```

```python
from contextlib import ExitStack

import numpy as np

import concourse.bass as bass
from concourse import mybir

F32 = mybir.dt.float32
BF16 = mybir.dt.bfloat16
F16 = mybir.dt.float16
I32 = mybir.dt.int32
U32 = mybir.dt.uint32
ALU = mybir.AluOpType
ACT = mybir.ActivationFunctionType
AX_X = mybir.AxisListType.X

P = 128
N = 6250
E = 200000
D = 64
H = 4
R = 4
WINDOWS = -(-N // P)
NP = WINDOWS * P
TILES = -(-E // P)
PAIRS = TILES + WINDOWS - 1
B = 8
BATCHES = 2 * (-(-PAIRS // (2 * B)))
TURNS = BATCHES // 2
GROUPS = -(-(BATCHES * B + 2 * B) // P)
KP = GROUPS * P
BE = B * P
FAR = 1 << 20
LN_EPS = 1e-5
ALPHA_EPS = 1e-9
WG = 7
NG = WINDOWS // WG
BANK = 512
AGG = D + 1
HA = H * D + H
T3 = 3 * D
Q3 = (1 + R) * D
BIG_NEG = -1.0e30
OW = WINDOWS + 1
O_TURNS = -(-TILES // (2 * B))
OT = O_TURNS * 2 * B

W_LIN1 = 0
W_OUT1 = W_LIN1 + H * D
W_ATT = W_OUT1 + H * D
W_EDGE_I = W_ATT + 2 * H
W_EDGE_J = W_EDGE_I + D
W_DST3 = W_EDGE_J + D
W_SRC3 = W_DST3 + Q3
W_COLS = W_SRC3 + Q3
V_OUT_B, V_LN_G, V_LN_B, V_EDGE_B, V_GAMMA, V_BETA, V_A3, V_WA_B, V_LIN3_B = range(9)
NVEC = 9

assert B * OW <= BANK and OT <= KP and KP - OT <= P
assert WINDOWS % WG == 0 and WG * AGG <= BANK
assert all((w * 37) >> 8 == w // WG for w in range(WINDOWS))


class Chain:

    def __init__(self, eng, sem, base=0):
        self.eng, self.sem, self.base, self.n = eng, sem, base, 0

    def __call__(self, ins):
        self.n += 1
        ins.then_inc(self.sem, 1)
        self.eng.wait_ge(self.sem, self.base + self.n)


def over_turns(eng, body):
    body(0)
    with eng.Fori(1, TURNS) as t:
        body(t)


def ring_free(eng, sem, b):
    if not (isinstance(b, int) and b < 2):
        eng.wait_ge(sem, b - 1)


def build(nc, x_in, edges, order_src, weights, vectors, lin3, out):
    outer = ExitStack()
    with outer:
        def keep(name, shape, dt=F32):
            return outer.enter_context(nc.sbuf_tensor(name, shape, dt))

        def dram(name, shape, dt):
            return nc.dram_tensor(name, shape, dt).ap()

        key_flat = dram("key_flat", (KP, P), BF16)
        key_flat1 = dram("key_flat1", (KP, P), BF16)
        by_src = dram("by_src", (KP, 2 * P), I32)
        code_flat = dram("code_flat", (KP, P), F16)
        att_table = dram("att_table", (NP, D + H), F32)
        edge_table = dram("edge_table", (NP, D), F32)
        gate_table = dram("gate_table", (R * NP, T3), F32)
        held = dram("held", (BATCHES * P, B * AGG), F32)
        score_flat = dram("score_flat", (KP, P), F32)
        weight_flat = dram("weight_flat", (KP, P), F32)

        X = keep("X", [P, WINDOWS * D])
        Wt = keep("Wt", [D, W_COLS])
        Vt = keep("Vt", [P, NVEC * D])
        L3 = keep("L3", [P, D])
        ident = keep("ident", [P, P])
        iotaF = keep("iotaF", [P, P])
        kcol = keep("kcol", [P, GROUPS])
        ones = keep("ones", [P, P], BF16)
        before = keep("before", [P, P], BF16)
        iotaT = keep("iotaT", [P, R])
        key = keep("key", [P, KP])
        valid = keep("valid", [P, KP])
        src_idx = keep("src_idx", [P, KP], U32)
        row_idx = keep("row_idx", [P, KP], U32)
        score = keep("score", [P, KP])
        w_row = keep("w_row", [P, KP], I32)
        a_row = keep("a_row", [P, KP], I32)
        deg = keep("deg", [P, WINDOWS])
        stat = keep("stat", [P, 2 * D])
        idx_now = keep("idx_now", [P, 2, B], U32)
        parts = keep("parts", [P, WINDOWS * 3 * Q3], BF16)
        PS = outer.enter_context(nc.psum_tensor("PS", [P, 8 * BANK], F32))

        part3 = parts[:, :].rearrange("p (w c f) -> p w c f", c=3, f=Q3)
        part2 = parts[:, 0:WINDOWS * 3 * D].rearrange("p (w c f) -> p w c f", c=3, f=D)
        sums1 = parts[:, 0:2 * WINDOWS * HA].bitcast(F32)
        part1 = parts[:, 2 * WINDOWS * HA:2 * WINDOWS * HA + WINDOWS * 3 * H] \
            .rearrange("p (w c f) -> p w c f", c=3, f=H)

        X3 = X[:, :].rearrange("p (w d) -> p w d", d=D)
        sums_psum = PS[:, 0:NG * BANK].rearrange("p (k c) -> p k c", c=BANK)[:, :, 0:WG * AGG] \
            .rearrange("p k (j f) -> p k j f", f=AGG)

        def bank(b, n=1):
            return PS[:, b * BANK:(b + n) * BANK]

        def vec(i):
            return Vt[:, i * D:(i + 1) * D]

        def rows_of(t, w):
            return t.unsqueeze(1).to_broadcast([P, w, D])

        paces = {e: outer.enter_context(nc.semaphore(f"pace_{e}")) for e in ("tensor", "gpsimd")}

        scattered = [outer.enter_context(nc.semaphore(f"scattered{s}")) for s in range(2)]
        pair_rows_in = {n: outer.enter_context(nc.semaphore(f"{n}_rows_in")) for n in ("by_dst", "by_src")}

        def hold(eng, which, sem, value):
            eng.wait_ge(sem, value)
            eng.sem_inc(paces[which], 1)

        spent = []

        def clear_spent():
            assert sorted(spent) == list(range(min(spent), max(spent) + 1))
            with nc.Block() as block:
                @block.sync
                def _(sp):
                    sp.sem_clear(range(min(spent), max(spent) + 1))
            spent.clear()

        class Phase:

            def __init__(self, name):
                self.name, self.ctx = name, ExitStack()

            def __enter__(self):
                self.ctx.__enter__()
                return self

            def __exit__(self, *a):
                return self.ctx.__exit__(*a)

            def sb(self, name, shape, dt=F32):
                return self.ctx.enter_context(nc.sbuf_tensor(f"{self.name}_{name}", shape, dt))

            def sem(self, name):
                new = self.ctx.enter_context(nc.semaphore(f"{self.name}_{name}"))
                assert new.num not in spent
                spent.append(new.num)
                return new

        def layer_norm(dve, link, src, dst, ph, tag):
            mean, var, centred, square, to_root, rooted = ph
            s3 = src.rearrange("p (w d) -> p w d", d=D)
            c3 = centred[:, :].rearrange("p (w d) -> p w d", d=D)
            d3 = dst.rearrange("p (w d) -> p w d", d=D)
            link(nc.vector.reduce_sum(mean[:, :], s3, AX_X))
            link(nc.vector.tensor_scalar(mean[:, :], mean[:, :], 1.0 / D, None, ALU.mult))
            link(nc.vector.tensor_tensor(c3, s3, mean[:, :].unsqueeze(2).to_broadcast([P, WINDOWS, D]),
                                         ALU.subtract))
            link(nc.vector.tensor_tensor(square[:, :], centred[:, :], centred[:, :], ALU.mult))
            link(nc.vector.reduce_sum(var[:, :], square[:, :].rearrange("p (w d) -> p w d", d=D), AX_X))
            nc.vector.tensor_scalar(var[:, :], var[:, :], 1.0 / D, LN_EPS, ALU.mult,
                                    ALU.add).then_inc(to_root, 1)
            dve.wait_ge(rooted, tag)
            link(nc.vector.reciprocal(var[:, :], var[:, :]))
            link(nc.vector.tensor_tensor(d3, c3, var[:, :].unsqueeze(2).to_broadcast([P, WINDOWS, D]),
                                         ALU.mult))

        def norm_tools(ph):
            return (ph.sb("mean", [P, WINDOWS]), ph.sb("var", [P, WINDOWS]), ph.sb("centred", [P, WINDOWS * D]),
                    ph.sb("square", [P, WINDOWS * D]), ph.sem("to_root"), ph.sem("rooted"))

        def take_root(act, tools, tag):
            _, var, _, _, to_root, rooted = tools
            act.wait_ge(to_root, tag)
            nc.scalar.activation(var[:, :], var[:, :], ACT.Sqrt).then_inc(rooted, 1)

        def split3(link, src, hi, mid, low, rest):
            link(nc.vector.tensor_copy(hi, src))
            link(nc.vector.tensor_tensor(rest, src, hi, ALU.subtract))
            link(nc.vector.tensor_copy(mid, rest))
            link(nc.vector.tensor_tensor(rest, rest, mid, ALU.subtract))
            link(nc.vector.tensor_copy(low, rest))

        def gather_rows(pool, table, ring, idx_ready, ring_used, rows_in):
            def turn(t):
                for s in range(2):
                    b = t * 2 + s
                    ring_free(pool, ring_used, b)
                    hold(pool, "gpsimd", idx_ready, b + 1)
                    for u in range(B):
                        pool.indirect_dma_start(
                            out=ring(s, u), out_offset=None, in_=table,
                            in_offset=bass.IndirectOffsetOnAxis(ap=idx_now[:, s, u:u + 1], axis=0),
                        ).then_inc(rows_in[s], 16)
            over_turns(pool, turn)

        def load_keys(sp, flat, ring, ring_used, keys_in):
            def turn(t):
                for s in range(2):
                    b = t * 2 + s
                    ring_free(sp, ring_used, b)
                    sp.dma_start(ring[:, s, :], flat.rearrange("k e -> (k e)").unsqueeze(0)
                                 [:, bass.ds(b * BE, BE)].to_broadcast([P, BE])).then_inc(keys_in[s], 16)
            over_turns(sp, turn)

        def part1_at(w, c):
            at = 2 * WINDOWS * HA
            return parts[:, bass.ds(w * (3 * H) + (at + c * H), H)]

        def part2_at(w, c):
            return parts[:, bass.ds(w * (3 * D) + c * D, D)]

        def put_indices(idx, b, s, idx_ready):
            nc.vector.tensor_copy(idx_now[:, s, :], idx[:, bass.ds(b * B, B)]).then_inc(idx_ready, 1)

        def one_hot_edges(OH, s, b, key=key):
            return nc.vector.tensor_tensor(
                OH[:, s], iotaF[:, :].unsqueeze(1).to_broadcast([P, B, P]),
                key[:, bass.ds(b * B, B)].unsqueeze(2).to_broadcast([P, B, P]), ALU.is_equal)

        def load_places(eng, row, b, bound):
            return [eng.value_load(row[0:1, bass.ds(b * B + u, 1)], min_val=0, max_val=bound)
                    for u in range(B)]

        A_MAX = (WINDOWS - 1) * AGG + (WINDOWS - 1) // WG * (BANK - WG * AGG)

        def add_up(pe, OH, s, u, a, rows, width):
            return nc.tensor.matmul(PS[:, bass.ds(a, width)], OH[:, s, u, :], rows, start=False,
                                    stop=True, skip_group_check=True)

        with Phase("start") as ph:
            iotaP = ph.sb("iotaP", [P, 1])
            loaded, consts = ph.sem("loaded"), ph.sem("consts")
            with nc.Block() as block:
                @block.sync
                def _(sp):
                    sp.dma_start(X3, x_in.rearrange("(w p) d -> p w d", p=P)).then_inc(loaded, 16)
                    sp.dma_start(Wt[:, :], weights).then_inc(loaded, 16)
                    sp.dma_start(L3[:, :], lin3).then_inc(loaded, 16)
                    sp.dma_start(Vt[:, :], vectors.to_broadcast([P, NVEC * D])).then_inc(loaded, 16)
                    sp.wait_ge(loaded, 64)

                @block.gpsimd
                def _(pool):
                    def count(t, pattern, mult):
                        pool.iota(t, pattern=pattern, base=0, channel_multiplier=mult,
                                  allow_small_or_imprecise_dtypes=True).then_inc(consts, 1)
                    count(kcol[:, :], [[P, GROUPS]], 1)
                    count(iotaF[:, :], [[1, P]], 0)
                    count(iotaP[:, :], [[0, 1]], 1)
                    count(iotaT[:, :], [[P, R]], 1)

                @block.vector
                def _(dve):
                    nc.vector.memset(ones[:, :], 1.0)
                    dve.wait_ge(consts, 4)
                    nc.vector.tensor_scalar(ident[:, :], iotaF[:, :], iotaP[:, :], None, ALU.is_equal)
                    nc.vector.tensor_scalar(before[:, :], iotaF[:, :], iotaP[:, :], None, ALU.is_gt)

        with Phase("order") as ph:
            raw = ph.sb("raw", [P, 2, GROUPS, P], I32)
            rawf = parts[:, 0:4 * KP].bitcast(F32).rearrange("p (f g e) -> p f g e", f=2, e=P)
            pay = ph.sb("pay", [P, KP, 2], I32)
            win = parts[:, 6 * KP:8 * KP].bitcast(F32)
            wini = parts[:, 4 * KP:6 * KP].bitcast(I32)
            fill = ph.sb("fill", [KP - OT, 2 * P], I32)
            OHW = ph.sb("OHW", [P, 2, B, OW], BF16)
            hist, upto, zero = ph.sb("hist", [P, OW]), ph.sb("upto", [P, OW]), ph.sb("zero", [P, OW])
            A = ph.sb("A", [P, 2, B + 1, OW])
            Q = ph.sb("Q", [P, 2, B, OW])
            placef = ph.sb("placef", [P, 2, B])
            pay_now = ph.sb("pay_now", [P, 2, B, 2], I32)
            loaded, rawf_ready, columns, filled = ph.sem("loaded"), ph.sem("rawf_ready"), ph.sem("columns"), ph.sem("filled")
            fill_out, seq, oh1, counted = ph.sem("fill_out"), ph.sem("seq"), ph.sem("oh1"), ph.sem("counted")
            oh2, ranked, q_ready, qseq = ph.sem("oh2"), ph.sem("ranked"), ph.sem("q_ready"), ph.sem("qseq")
            place_ready, zeroed = ph.sem("place_ready"), ph.sem("zeroed")

            def windows_of(s, b):
                return nc.vector.tensor_tensor(
                    OHW[:, s], iotaF[:, 0:OW].unsqueeze(1).to_broadcast([P, B, OW]),
                    win[:, bass.ds(b * B, B)].unsqueeze(2).to_broadcast([P, B, OW]), ALU.is_equal)

            with nc.Block() as block:
                @block.sync
                def _(sp):
                    sp.dma_start(raw[:, 0], order_src.rearrange("(g p) e -> p g e", p=P)).then_inc(loaded, 16)
                    sp.dma_start(raw[:, 1], edges.rearrange("(g p) c -> p g c", p=P)[:, :, P:2 * P]).then_inc(loaded, 16)
                    sp.wait_ge(filled, 1)
                    sp.dma_start(by_src[OT:KP, :], fill[:, :]).then_inc(fill_out, 16)
                    sp.wait_ge(fill_out, 16)

                @block.gpsimd
                def _(pool):
                    to = by_src.rearrange("t (e f) -> (t e) f", f=2)

                    def turn(t):
                        for s in range(2):
                            b = t * 2 + s
                            hold(pool, "gpsimd", place_ready, b + 1)
                            for u in range(B):
                                pool.indirect_dma_start(
                                    out=to, out_offset=bass.IndirectOffsetOnAxis(ap=idx_now[:, s, u:u + 1], axis=0),
                                    in_=pay_now[:, s, u, :], in_offset=None).then_inc(scattered[s], 16)
                    turn(0)
                    with pool.Fori(1, O_TURNS) as t:
                        turn(t)
                    for s in range(2):
                        pool.wait_ge(scattered[s], P * O_TURNS)

                @block.tensor
                def _(pe):
                    pe.wait_ge(rawf_ready, 1)
                    for f in range(2):
                        for g in range(GROUPS):
                            at = f * 4 * BANK + g * P
                            ins = nc.tensor.transpose(PS[:, at:at + P], rawf[:, f, g, :], ident[:, :])
                    ins.then_inc(columns, 1)
                    pe.wait_ge(zeroed, 1)

                    def count(t):
                        for s in range(2):
                            b = t * 2 + s
                            pe.wait_ge(oh1, b + 1)
                            nc.tensor.matmul(bank(4)[:, 0:B * OW], ones[:, :], OHW[:, s].rearrange("p t w -> p (t w)"),
                                             start=False, stop=True, skip_group_check=True).then_inc(counted, 1)
                    count(0)
                    with pe.Fori(1, O_TURNS) as t:
                        count(t)

                    def rank(t):
                        for s in range(2):
                            b = t * 2 + s
                            pe.wait_ge(oh2, b + 1)
                            ring_free(pe, q_ready, b)
                            oh = OHW[:, s].rearrange("p t w -> p (t w)")
                            nc.tensor.matmul(bank(s)[:, 0:B * OW], before[:, :], oh, start=True, stop=True)
                            nc.tensor.matmul(bank(2 + s)[:, 0:B * OW], ones[:, :], oh, start=True,
                                             stop=True).then_inc(ranked, 1)
                    rank(0)
                    with pe.Fori(1, O_TURNS) as t:
                        rank(t)

                @block.vector
                def _(dve):
                    link = Chain(dve, seq)
                    nc.vector.memset(fill[:, :], FAR).then_inc(filled, 1)
                    dve.wait_ge(loaded, 32)
                    nc.vector.tensor_copy(rawf[:, :, :, :], raw[:, :, :, :]).then_inc(rawf_ready, 1)
                    dve.wait_ge(columns, 1)
                    link(nc.vector.tensor_copy(pay[:, :, 0], PS[:, 0:KP]))
                    link(nc.vector.tensor_copy(pay[:, :, 1], PS[:, 4 * BANK:4 * BANK + KP]))
                    link(nc.vector.tensor_scalar(wini[:, :], pay[:, :, 0], 7, None, ALU.arith_shift_right))
                    link(nc.vector.tensor_copy(win[:, :], wini[:, :]))
                    nc.vector.memset(bank(4), 0.0).then_inc(zeroed, 1)

                    def count(t):
                        for s in range(2):
                            b = t * 2 + s
                            ring_free(dve, counted, b)
                            windows_of(s, b).then_inc(oh1, 1)
                    count(0)
                    with dve.Fori(1, O_TURNS) as t:
                        count(t)
                    dve.wait_ge(counted, 2 * O_TURNS)
                    link(nc.vector.reduce_sum(hist[:, :], bank(4)[:, 0:B * OW].rearrange("p (t w) -> p w t", w=OW), AX_X))
                    link(nc.vector.memset(zero[:, :], 0.0))
                    link(nc.vector.tensor_tensor_scan(upto[:, :], hist[:, :], zero[:, :], 0.0, ALU.add, ALU.add))
                    link(nc.vector.tensor_tensor(A[:, 1, B, :], upto[:, :], hist[:, :], ALU.subtract))

                    def place(t):
                        for s in range(2):
                            b = t * 2 + s
                            ql = Chain(dve, qseq, b * (B + 4))
                            windows_of(s, b).then_inc(oh2, 1)
                            ql(nc.vector.tensor_copy(A[:, s, 0, :], A[:, 1 - s, B, :]))
                            dve.wait_ge(ranked, b + 1)
                            tot = bank(2 + s)[:, 0:B * OW].rearrange("p (t w) -> p t w", w=OW)
                            for u in range(B):
                                ql(nc.vector.tensor_tensor(A[:, s, u + 1, :], A[:, s, u, :], tot[:, u, :], ALU.add))
                            ql(nc.vector.tensor_tensor(Q[:, s], bank(s)[:, 0:B * OW].rearrange("p (t w) -> p t w", w=OW),
                                                       A[:, s, 0:B, :], ALU.add))
                            nc.vector.tensor_tensor(Q[:, s], Q[:, s], OHW[:, s], ALU.mult).then_inc(q_ready, 1)
                            dve.wait_ge(q_ready, b + 1)
                            ql(nc.vector.reduce_sum(placef[:, s, :], Q[:, s], AX_X))
                            if not (isinstance(b, int) and b < 2):
                                dve.wait_ge(scattered[s], P * t)
                            ql(nc.vector.tensor_copy(idx_now[:, s, :], placef[:, s, :]))
                            nc.vector.tensor_copy(pay_now[:, s], pay[:, bass.ds(b * B, B), :]).then_inc(place_ready, 1)
                    place(0)
                    with dve.Fori(1, O_TURNS) as t:
                        place(t)

        def pair_up(name, table, fields_n, interleaved, key, gather_idx, w_row, key_to, typed):
            ph = Phase(name)
            with ph:
                pair_up_in(ph, table, fields_n, interleaved, key, gather_idx, w_row, key_to, typed)

        def pair_up_in(ph, table, fields_n, interleaved, key, gather_idx, w_row, key_to, typed):
            last = ph.sb("last", [P, GROUPS], I32)
            wl = ph.sb("wl", [P, GROUPS], I32)
            ends = ph.sb("ends", [P, GROUPS])
            past = parts[:, 0:GROUPS * KP].rearrange("p (g k) -> p g k", k=KP)
            iotaK = parts[:, GROUPS * KP:(GROUPS + 2) * KP].bitcast(F32)
            wbc = ph.sb("wbc", [P, KP])
            sev = ph.sb("sev", [P, KP], I32)
            tcol = ph.sb("tcol", [P, GROUPS], U32)
            wcol = ph.sb("wcol", [P, GROUPS])
            rows_i = ph.sb("rows_i", [P, GROUPS, fields_n * P], I32)
            last_in, consts = ph.sem("last_in"), ph.sem("consts")
            seq, past_ready, counted = ph.sem("seq"), ph.sem("past_ready"), ph.sem("counted")
            tiles_ready, rows_in = ph.sem("tiles_ready"), pair_rows_in[ph.name]
            with nc.Block() as block:
                @block.sync
                def _(sp):
                    sp.dma_start(last[:, :].unsqueeze(2),
                                 table.rearrange("(g p) c -> p g c", p=P)[:, :, 2 * P - 2:2 * P - 1] if interleaved
                                 else table.rearrange("(g p) c -> p g c", p=P)[:, :, 2 * P - 1:2 * P],
                                 allow_slow_non_contiguous=True).then_inc(last_in, 16)

                @block.gpsimd
                def _(pool):
                    def count(t, pattern, mult):
                        pool.iota(t, pattern=pattern, base=0, channel_multiplier=mult,
                                  allow_small_or_imprecise_dtypes=True).then_inc(consts, 1)
                    count(iotaK[:, :], [[1, KP]], 0)
                    pool.wait_ge(tiles_ready, 1)
                    for g in range(GROUPS):
                        pool.indirect_dma_start(
                            out=rows_i[:, g, :], out_offset=None, in_=table,
                            in_offset=bass.IndirectOffsetOnAxis(ap=tcol[:, g:g + 1], axis=0)).then_inc(rows_in, 16)
                    pool.wait_ge(rows_in, 16 * GROUPS)

                @block.vector
                def _(dve):
                    link = Chain(dve, seq)
                    nc.vector.memset(score[:, :], 0.0)
                    dve.wait_ge(consts, 1)
                    dve.wait_ge(last_in, 16)
                    link(nc.vector.tensor_scalar(wl[:, :], last[:, :], 7, None, ALU.arith_shift_right))
                    link(nc.vector.tensor_scalar(ends[:, :], wl[:, :], float(WINDOWS - 1), None, ALU.min))
                    link(nc.vector.tensor_tensor(ends[:, :], ends[:, :], kcol[:, :], ALU.add))
                    for g in range(GROUPS):
                        ins = nc.vector.tensor_scalar(past[:, g, :], iotaK[:, :], ends[:, g:g + 1], None, ALU.is_gt)
                    ins.then_inc(past_ready, 1)
                    dve.wait_ge(counted, 1)
                    link(nc.vector.tensor_copy(wcol[:, :], bank(4)[:, 0:GROUPS]))
                    nc.vector.tensor_copy(tcol[:, :], wcol[:, :]).then_inc(tiles_ready, 1)
                    dve.wait_ge(tiles_ready, 1)
                    link(nc.vector.tensor_tensor(wcol[:, :], kcol[:, :], wcol[:, :], ALU.subtract))
                    link(nc.vector.tensor_scalar(wcol[:, :], wcol[:, :], float(WINDOWS - 1), float(P), ALU.min, ALU.mult))
                    c4 = KP // 4
                    for c in range(4):
                        ins = nc.vector.tensor_tensor(wbc[:, c * c4:(c + 1) * c4], iotaK[:, c * c4:(c + 1) * c4],
                                                      bank(c)[:, 0:c4], ALU.subtract)
                    link(ins)
                    link(nc.vector.tensor_scalar(wbc[:, :], wbc[:, :], float(WINDOWS - 1), None, ALU.min))
                    link(nc.vector.tensor_copy(w_row, wbc[:, :]))
                    if typed:
                        link(nc.vector.tensor_scalar(sev[:, :], wbc[:, :], 37.0, None, ALU.mult))
                        link(nc.vector.tensor_scalar(sev[:, :], sev[:, :], 8, None, ALU.arith_shift_right))
                        link(nc.vector.tensor_scalar(a_row[:, :], sev[:, :], float(BANK - WG * AGG), None, ALU.mult))
                        link(nc.vector.scalar_tensor_tensor(a_row[:, :], wbc[:, :], float(AGG), a_row[:, :],
                                                            ALU.mult, ALU.add))
                    link(nc.vector.tensor_scalar(key, wbc[:, :], float(P), None, ALU.mult))

                @block.tensor
                def _(pe):
                    pe.wait_ge(past_ready, 1)
                    c4 = KP // 4
                    for c in range(4):
                        for g in range(GROUPS):
                            nc.tensor.matmul(bank(c)[:, 0:c4], ones[:, :], past[:, g, c * c4:(c + 1) * c4],
                                             start=(g == 0), stop=(g == GROUPS - 1))
                    for j in range(GROUPS):
                        for g in range(GROUPS):
                            ins = nc.tensor.matmul(bank(4)[:, j:j + 1], past[:, g, j * P:(j + 1) * P], ones[:, 0:1],
                                                   start=(g == 0), stop=(g == GROUPS - 1))
                    ins.then_inc(counted, 1)

            spare = parts[:, 0:12 * KP].bitcast(F32).rearrange("p (f g e) -> p f g e", g=GROUPS, e=P)
            fields, key_r, inside, hit = spare[:, 0:3], spare[:, 3], spare[:, 4], spare[:, 5]
            key_b = ph.sb("key_b", [P, GROUPS, P], BF16)
            code_h = ph.sb("code_h", [P, GROUPS, P], F16)
            seq2, fields_ready, rows_done = ph.sem("seq2"), ph.sem("fields_ready"), ph.sem("rows_done")
            columns, taken, stored = ph.sem("columns"), ph.sem("taken"), ph.sem("stored")
            with nc.Block() as block:
                @block.sync
                def _(sp):
                    sp.wait_ge(rows_done, 1 + typed)
                    sp.dma_start(key_to.rearrange("(g p) e -> p g e", p=P), key_b[:, :, :]).then_inc(stored, 16)
                    if typed:
                        sp.dma_start(code_flat.rearrange("(g p) e -> p g e", p=P), code_h[:, :, :]).then_inc(stored, 16)
                    sp.wait_ge(stored, 16 + 16 * typed)

                @block.vector
                def _(dve):
                    link = Chain(dve, seq2)
                    for f in range(fields_n):
                        from_ = rows_i[:, :, :].rearrange("p g (e f) -> p g f e", f=2)[:, :, 1 - f, :] \
                            if interleaved else rows_i[:, :, f * P:(f + 1) * P]
                        ins = nc.vector.tensor_copy(fields[:, f], from_)
                    ins.then_inc(fields_ready, 1)
                    dve.wait_ge(fields_ready, 1)
                    wb = wcol[:, :].unsqueeze(2).to_broadcast([P, GROUPS, P])
                    link(nc.vector.tensor_tensor(key_r[:, :, :], fields[:, 1], wb, ALU.subtract))
                    link(nc.vector.tensor_scalar(key_r[:, :, :], key_r[:, :, :], -1.0, float(P), ALU.max, ALU.min))
                    nc.vector.tensor_copy(key_b[:, :, :], key_r[:, :, :]).then_inc(rows_done, 1)
                    if typed:
                        link(nc.vector.tensor_scalar(inside[:, :, :], key_r[:, :, :], 0.0, None, ALU.is_ge))
                        link(nc.vector.tensor_scalar(hit[:, :, :], key_r[:, :, :], float(P), None, ALU.is_lt))
                        link(nc.vector.tensor_tensor(inside[:, :, :], inside[:, :, :], hit[:, :, :], ALU.mult))
                        link(nc.vector.scalar_tensor_tensor(key_r[:, :, :], fields[:, 2], float(P), key_r[:, :, :],
                                                            ALU.mult, ALU.add))
                        link(nc.vector.scalar_tensor_tensor(key_r[:, :, :], key_r[:, :, :], 1.0, inside[:, :, :],
                                                            ALU.add, ALU.mult))
                        nc.vector.tensor_scalar(code_h[:, :, :], key_r[:, :, :], -1.0, None,
                                                ALU.add).then_inc(rows_done, 1)
                    dve.wait_ge(columns, 1)
                    nc.vector.tensor_scalar(gather_idx, PS[:, 0:KP], float(NP - 1), None, ALU.min).then_inc(taken, 1)
                    dve.wait_ge(columns, 2)
                    link(nc.vector.tensor_tensor(key, PS[:, 4 * BANK:4 * BANK + KP], key, ALU.subtract))
                    link(nc.vector.tensor_scalar(key, key, -1.0, float(P), ALU.max, ALU.min))
                    if typed:
                        link(nc.vector.tensor_scalar(valid[:, :], key, 0.0, None, ALU.is_ge))
                        link(nc.vector.tensor_scalar(wbc[:, :], key, float(P), None, ALU.is_lt))
                        link(nc.vector.tensor_tensor(valid[:, :], valid[:, :], wbc[:, :], ALU.mult))
                        dve.wait_ge(taken, 1)
                        dve.wait_ge(columns, 3)
                        link(nc.vector.scalar_tensor_tensor(row_idx[:, :], PS[:, 0:KP], float(NP), gather_idx,
                                                            ALU.mult, ALU.add))

                @block.tensor
                def _(pe):
                    pe.wait_ge(fields_ready, 1)
                    for f in range(fields_n):
                        if f == 2:
                            pe.wait_ge(taken, 1)
                        for g in range(GROUPS):
                            at = (f % 2) * 4 * BANK + g * P
                            ins = nc.tensor.transpose(PS[:, at:at + P], fields[:, f, g, :], ident[:, :])
                        ins.then_inc(columns, 1)

        by_src_key, by_src_idx, by_src_w = (
            parts[:, WINDOWS * 3 * Q3 - (i + 1) * 2 * KP:WINDOWS * 3 * Q3 - i * 2 * KP].bitcast(dt)
            for i, dt in enumerate((F32, U32, I32)))
        pair_up("by_dst", edges, 3, False, key[:, :], src_idx[:, :], w_row[:, :], key_flat, True)
        pair_up("by_src", by_src, 2, True, by_src_key, by_src_idx, by_src_w, key_flat1, False)
        clear_spent()

        with Phase("mean") as ph:
            G = ph.sb("G", [P, 2, B, AGG])
            OH = ph.sb("OH", [P, 2, B, P])
            idx_ready, oh_ready, agg_done = ph.sem("idx_ready"), ph.sem("oh_ready"), ph.sem("agg_done")
            rows_in = [ph.sem(f"rows_in{s}") for s in range(2)]
            zeroed = ph.sem("zeroed")
            with nc.Block() as block:
                @block.gpsimd
                def _(pool):
                    gather_rows(pool, x_in, lambda s, u: G[:, s, u, 0:D], idx_ready, agg_done, rows_in)

                @block.vector
                def _(dve):
                    put_indices(src_idx, 0, 0, idx_ready)
                    put_indices(src_idx, 1, 1, idx_ready)
                    nc.vector.memset(PS[:, 0:NG * BANK], 0.0).then_inc(zeroed, 1)
                    nc.vector.memset(G[:, :, :, D:AGG], 1.0).then_inc(zeroed, 1)

                    def turn(t):
                        for s in range(2):
                            b = t * 2 + s
                            ring_free(dve, agg_done, b)
                            one_hot_edges(OH, s, b).then_inc(oh_ready, 1)
                            dve.wait_ge(rows_in[s], P * (t + 1))
                            put_indices(src_idx, b + 2, s, idx_ready)
                    over_turns(dve, turn)

                @block.tensor
                def _(pe):
                    pe.wait_ge(zeroed, 2)

                    def turn(t):
                        for s in range(2):
                            b = t * 2 + s
                            at = load_places(pe, a_row, b, A_MAX)
                            pe.wait_ge(oh_ready, b + 1)
                            pe.wait_ge(rows_in[s], P * (t + 1))
                            for u in range(B):
                                ins = add_up(pe, OH, s, u, at[u], G[:, s, u, :], AGG)
                            ins.then_inc(agg_done, 1)
                    over_turns(pe, turn)

        with Phase("node1") as ph:
            Y = ph.sb("Y", [P, WINDOWS * D])
            Y3 = Y[:, :].rearrange("p (w d) -> p w d", d=D)
            inv = ph.sb("inv", [P, WINDOWS])
            WA = ph.sb("WA", [D, 2 * H])
            stage = ph.sb("stage", [P, WG, D])
            XT = ph.sb("XT", [D, WG * P])
            TAB = ph.sb("TAB", [P, WG, D + H])
            rest = ph.sb("rest", [P, WG, H])
            full = ph.sb("full", [P, WG, H])
            tools = norm_tools(ph)
            seq, wa_done, wa_ready = ph.sem("seq"), ph.sem("wa_done"), ph.sem("wa_ready")
            staged, turned, xt_ready, made = ph.sem("staged"), ph.sem("turned"), ph.sem("xt_ready"), ph.sem("made")
            gseq, tab_ready, stored = ph.sem("gseq"), ph.sem("tab_ready"), ph.sem("stored")
            with nc.Block() as block:
                @block.scalar
                def _(act):
                    take_root(act, tools, 1)
                    with act.Fori(0, NG) as g:
                        act.wait_ge(turned, g + 1)
                        nc.scalar.copy(XT[:, :], PS[0:D, 0:WG * P]).then_inc(xt_ready, 1)

                @block.vector
                def _(dve):
                    link = Chain(dve, seq)
                    link(nc.vector.tensor_copy(deg[:, :].rearrange("p (k j) -> p k j", j=WG), sums_psum[:, :, :, D]))
                    link(nc.vector.tensor_scalar(deg[:, :], deg[:, :], 1.0, None, ALU.max))
                    link(nc.vector.reciprocal(inv[:, :], deg[:, :]))
                    for k in range(NG):
                        ins = nc.vector.tensor_tensor(
                            Y3[:, k * WG:(k + 1) * WG, :], sums_psum[:, k, :, 0:D],
                            inv[:, k * WG:(k + 1) * WG].unsqueeze(2).to_broadcast([P, WG, D]), ALU.mult)
                    link(ins)
                    link(nc.vector.tensor_tensor(Y[:, :], Y[:, :], X[:, :], ALU.add))
                    layer_norm(dve, link, Y[:, :], X[:, :], tools, 1)
                    nc.vector.memset(sums1[:, :], 0.0)
                    dve.wait_ge(wa_done, 1)
                    nc.vector.tensor_copy(WA[:, :], bank(7)[0:D, 0:2 * H]).then_inc(wa_ready, 1)
                    with dve.Fori(0, NG) as g:
                        gl = Chain(dve, gseq, g * 5)
                        nc.vector.tensor_copy(stage[:, :, :], X3[:, bass.ds(g * WG, WG), :]).then_inc(staged, 1)
                        dve.wait_ge(made, g + 1)
                        m3 = bank(2)[:, 0:WG * 2 * H].rearrange("p (j f) -> p j f", f=2 * H)
                        nc.vector.tensor_copy(TAB[:, :, 0:D], stage[:, :, :])
                        nc.vector.tensor_copy(TAB[:, :, D:D + H], m3[:, :, 0:H]).then_inc(tab_ready, 1)
                        w = bass.ds(g * WG, WG)
                        split3(gl, m3[:, :, H:2 * H], part1[:, w, 0, :], part1[:, w, 1, :], part1[:, w, 2, :],
                               rest[:, :, :])
                        dve.wait_ge(stored, g * 16 + 16)

                @block.sync
                def _(sp):
                    with sp.Fori(0, NG) as g:
                        sp.wait_ge(tab_ready, g + 1)
                        sp.dma_start(att_table[bass.ds(g * (WG * P), WG * P), :].rearrange("(j p) f -> p j f", p=P),
                                     TAB[:, :, :]).then_inc(stored, 16)
                    sp.wait_ge(stored, 16 * NG)

                @block.tensor
                def _(pe):
                    for c in range(2 * H):
                        h = c % H
                        ins = nc.tensor.matmul(bank(7)[0:D, c:c + 1],
                                               Wt[:, W_LIN1 + h * D:W_LIN1 + (h + 1) * D],
                                               Wt[:, W_ATT + c:W_ATT + c + 1], start=True, stop=True)
                    ins.then_inc(wa_done, 1)
                    pe.wait_ge(wa_ready, 1)
                    with pe.Fori(0, NG) as g:
                        hold(pe, "tensor", staged, g + 1)
                        for j in range(WG):
                            ins = nc.tensor.transpose(PS[0:D, j * P:(j + 1) * P], stage[:, j, :], ident[:, :])
                        ins.then_inc(turned, 1)
                        pe.wait_ge(xt_ready, g + 1)
                        for j in range(WG):
                            ins = nc.tensor.matmul(bank(2)[:, j * 2 * H:(j + 1) * 2 * H], XT[:, j * P:(j + 1) * P],
                                                   WA[:, :], start=True, stop=True)
                        ins.then_inc(made, 1)

        with Phase("attention") as ph:
            G = ph.sb("G", [P, 2, B, D + H])
            OH = ph.sb("OH", [P, 2, B, P])
            KEYS = ph.sb("KEYS", [P, 2, BE], BF16)
            OHT = ph.sb("OHT", [P, 2, B, P], BF16)
            AL = ph.sb("AL", [P, 2, B, H])
            MSG = ph.sb("MSG", [P, 2, B, HA])
            keys_in = [ph.sem(f"keys_in{s}") for s in range(2)]
            rows_in = [ph.sem(f"rows_in{s}") for s in range(2)]
            idx_ready, oh_ready, oht_ready = ph.sem("idx_ready"), ph.sem("oh_ready"), ph.sem("oht_ready")
            dst_done, al_ready, exp_ready = ph.sem("dst_done"), ph.sem("al_ready"), ph.sem("exp_ready")
            msg_ready, agg_done, added, seq = ph.sem("msg_ready"), ph.sem("agg_done"), ph.sem("added"), ph.sem("seq")
            with nc.Block() as block:
                @block.sync
                def _(sp):
                    load_keys(sp, key_flat1, KEYS, oht_ready, keys_in)

                @block.gpsimd
                def _(pool):
                    gather_rows(pool, att_table, lambda s, u: G[:, s, u, :], idx_ready, msg_ready, rows_in)

                @block.scalar
                def _(act):
                    def turn(t):
                        for s in range(2):
                            b = t * 2 + s
                            act.wait_ge(al_ready, b + 1)
                            nc.scalar.activation(MSG[:, s, :, H * D:HA], AL[:, s, :, :],
                                                 ACT.Exp).then_inc(exp_ready, 1)
                    over_turns(act, turn)

                @block.vector
                def _(dve):
                    put_indices(by_src_idx, 0, 0, idx_ready)
                    put_indices(by_src_idx, 1, 1, idx_ready)

                    def take_sums(b, s, places):
                        for u in range(B):
                            dve.wait_ge(agg_done, b * B + u + 1)
                            to = sums1[:, bass.ds(places[u] * HA, HA)]
                            if not (isinstance(b, int) and b * B + u == 0):
                                dve.wait_ge(added, b * B + u)
                            nc.vector.tensor_tensor(to, to, bank(4 + u % 4)[:, 0:HA], ALU.add).then_inc(added, 1)

                    def turn(t):
                        for s in range(2):
                            b = t * 2 + s
                            link = Chain(dve, seq, b)
                            dve.wait_ge(keys_in[s], 16 * (t + 1))
                            ring_free(dve, dst_done, b)
                            nc.vector.tensor_scalar(OHT[:, s].rearrange("p b e -> p (b e)"), KEYS[:, s, :],
                                                    iotaT[:, 0:1], None, ALU.is_equal).then_inc(oht_ready, 1)
                            if not (isinstance(b, int) and b < 2):
                                dve.wait_ge(agg_done, (b - 1) * B)
                            one_hot_edges(OH, s, b, by_src_key).then_inc(oh_ready, 1)
                            dve.wait_ge(rows_in[s], P * (t + 1))
                            put_indices(by_src_idx, b + 2, s, idx_ready)
                            dve.wait_ge(dst_done, b + 1)
                            z = bank(s)[:, 0:B * H].rearrange("p (b h) -> p b h", h=H)
                            link(nc.vector.tensor_tensor(AL[:, s], z, G[:, s, :, D:D + H], ALU.add))
                            nc.vector.scalar_tensor_tensor(AL[:, s], AL[:, s], 0.2, AL[:, s], ALU.mult,
                                                           ALU.max).then_inc(al_ready, 1)
                            if not (isinstance(b, int) and b == 0):
                                take_sums(b - 1, 1 - s, load_places(dve, by_src_w, b - 1, WINDOWS - 1))
                            dve.wait_ge(exp_ready, b + 1)
                            nc.vector.tensor_tensor(
                                MSG[:, s, :, 0:H * D].rearrange("p b (h d) -> p b h d", d=D),
                                G[:, s, :, 0:D].unsqueeze(2).to_broadcast([P, B, H, D]),
                                MSG[:, s, :, H * D:HA].unsqueeze(3).to_broadcast([P, B, H, D]),
                                ALU.mult).then_inc(msg_ready, 1)
                    over_turns(dve, turn)
                    take_sums(BATCHES - 1, 1, load_places(dve, by_src_w, BATCHES - 1, WINDOWS - 1))

                @block.tensor
                def _(pe):
                    def turn(t):
                        for s in range(2):
                            b = t * 2 + s
                            at = load_places(pe, by_src_w, b, WINDOWS - 1)
                            pe.wait_ge(oht_ready, b + 1)
                            ring_free(pe, al_ready, b)
                            for u in range(B):
                                for c in range(3):
                                    ins = nc.tensor.matmul(bank(s)[:, u * H:(u + 1) * H], OHT[:, s, u, :],
                                                           part1_at(at[u], c), start=(c == 0), stop=(c == 2))
                            ins.then_inc(dst_done, 1)
                            if not (isinstance(b, int) and b == 0):
                                sum_heads(b - 1, 1 - s)

                    def sum_heads(b, s):
                        pe.wait_ge(oh_ready, b + 1)
                        pe.wait_ge(msg_ready, b + 1)
                        for u in range(B):
                            if not (isinstance(b, int) and b * B + u < 4):
                                pe.wait_ge(added, b * B + u - 3)
                            nc.tensor.matmul(bank(4 + u % 4)[:, 0:HA], OH[:, s, u, :], MSG[:, s, u, :],
                                             start=True, stop=True).then_inc(agg_done, 1)
                    over_turns(pe, turn)
                    sum_heads(BATCHES - 1, 1)

        with Phase("node2") as ph:
            Y = ph.sb("Y", [P, WINDOWS * D])
            Y3 = Y[:, :].rearrange("p (w d) -> p w d", d=D)
            inv = ph.sb("inv", [P, WINDOWS, H])
            C1 = ph.sb("C1", [D, H, D])
            stage = ph.sb("stage", [P, WG, H, D])
            XT = parts[0:D, WINDOWS * 3 * Q3 - 2 * H * WG * P:].bitcast(F32).rearrange("p (h k) -> p h k", h=H)
            tools = norm_tools(ph)
            seq, c_done, c_ready = ph.sem("seq"), ph.sem("c_done"), ph.sem("c_ready")
            staged, turned, xt_ready = ph.sem("staged"), ph.sem("turned"), ph.sem("xt_ready")
            made, gseq, neg_ready, exp_ready = ph.sem("made"), ph.sem("gseq"), ph.sem("neg_ready"), ph.sem("exp_ready")
            with nc.Block() as block:
                @block.scalar
                def _(act):
                    with act.Fori(0, NG) as g:
                        for h in range(H):
                            act.wait_ge(turned, g * H + (h + 1))
                            nc.scalar.copy(XT[:, h, :], PS[0:D, (h % 3) * 2 * BANK:(h % 3) * 2 * BANK + WG * P]) \
                                .then_inc(xt_ready, 1)
                    act.wait_ge(neg_ready, 1)
                    nc.scalar.activation(tools[3][:, :], tools[3][:, :], ACT.Exp).then_inc(exp_ready, 1)
                    take_root(act, tools, 1)
                    take_root(act, tools, 2)

                @block.vector
                def _(dve):
                    link = Chain(dve, seq)
                    dve.wait_ge(c_done, 1)
                    nc.vector.tensor_copy(C1[:, :, :].rearrange("k h o -> k (h o)"),
                                          bank(7)[0:D, 0:H * D]).then_inc(c_ready, 1)
                    dens = sums1.rearrange("p (w c) -> p w c", c=HA)[:, :, H * D:HA]
                    link(nc.vector.tensor_scalar(inv[:, :, :], dens, ALPHA_EPS, None, ALU.add))
                    link(nc.vector.reciprocal(inv[:, :, :], inv[:, :, :]))
                    s4 = sums1.rearrange("p (w c) -> p w c", c=HA)[:, :, 0:H * D]
                    with dve.Fori(0, NG) as g:
                        w = bass.ds(g * WG, WG)
                        nc.vector.tensor_tensor(
                            stage[:, :, :, :], s4[:, w, :].rearrange("p w (h d) -> p w h d", d=D),
                            inv[:, w, :].unsqueeze(3).to_broadcast([P, WG, H, D]), ALU.mult).then_inc(staged, 1)
                        dve.wait_ge(made, g + 1)
                        nc.vector.tensor_tensor(Y3[:, w, :], bank(6)[:, 0:WG * D].rearrange("p (j d) -> p j d", d=D),
                                                rows_of(vec(V_OUT_B), WG), ALU.add).then_inc(gseq, 1)
                    dve.wait_ge(gseq, NG)
                    low = tools[3]
                    nc.vector.tensor_scalar(low[:, :], Y[:, :], 0.0, None, ALU.min).then_inc(neg_ready, 1)
                    dve.wait_ge(exp_ready, 1)
                    link(nc.vector.tensor_scalar(low[:, :], low[:, :], -1.0, None, ALU.add))
                    link(nc.vector.scalar_tensor_tensor(Y[:, :], Y[:, :], 0.0, low[:, :], ALU.max, ALU.add))
                    link(nc.vector.tensor_tensor(Y[:, :], Y[:, :], X[:, :], ALU.add))
                    layer_norm(dve, link, Y[:, :], Y[:, :], tools, 1)
                    link(nc.vector.tensor_tensor(Y3, Y3, rows_of(vec(V_LN_G), WINDOWS), ALU.mult))
                    link(nc.vector.tensor_tensor(Y3, Y3, rows_of(vec(V_LN_B), WINDOWS), ALU.add))
                    link(nc.vector.tensor_tensor(Y[:, :], Y[:, :], X[:, :], ALU.add))
                    layer_norm(dve, link, Y[:, :], X[:, :], tools, 2)

                @block.tensor
                def _(pe):
                    for h in range(H):
                        ins = nc.tensor.matmul(bank(7)[0:D, h * D:(h + 1) * D],
                                               Wt[:, W_LIN1 + h * D:W_LIN1 + (h + 1) * D],
                                               Wt[:, W_OUT1 + h * D:W_OUT1 + (h + 1) * D], start=True, stop=True)
                    ins.then_inc(c_done, 1)
                    pe.wait_ge(c_ready, 1)
                    with pe.Fori(0, NG) as g:
                        hold(pe, "tensor", staged, g + 1)
                        for h in range(H):
                            if h == 3:
                                hold(pe, "tensor", xt_ready, g * H + 1)
                            for j in range(WG):
                                at = (h % 3) * 2 * BANK + j * P
                                ins = nc.tensor.transpose(PS[0:D, at:at + P], stage[:, j, h, :], ident[:, :])
                            ins.then_inc(turned, 1)
                        pe.wait_ge(xt_ready, g * H + H)
                        for j in range(WG):
                            for h in range(H):
                                ins = nc.tensor.matmul(bank(6)[:, j * D:(j + 1) * D], XT[:, h, j * P:(j + 1) * P],
                                                       C1[:, h, :], start=(h == 0), stop=(h == H - 1))
                        ins.then_inc(made, 1)

        with Phase("tables2") as ph:
            WE = ph.sb("WE", [D, 2 * D])
            stage = ph.sb("stage", [P, WG, D])
            XT = ph.sb("XT", [D, WG * P])
            TAB = ph.sb("TAB", [P, WG, D])
            full = ph.sb("full", [P, WG, D])
            rest = ph.sb("rest", [P, WG, D])
            we_ready, staged, turned = ph.sem("we_ready"), ph.sem("staged"), ph.sem("turned")
            xt_ready, made, gseq = ph.sem("xt_ready"), ph.sem("made"), ph.sem("gseq")
            tab_ready, stored = ph.sem("tab_ready"), ph.sem("stored")
            pq = PS[:, 2 * BANK:2 * BANK + WG * 2 * D].rearrange("p (j f) -> p j f", f=2 * D)
            with nc.Block() as block:
                @block.sync
                def _(sp):
                    with sp.Fori(0, NG) as g:
                        sp.wait_ge(tab_ready, g + 1)
                        sp.dma_start(edge_table[bass.ds(g * (WG * P), WG * P), :].rearrange("(j p) f -> p j f", p=P),
                                     TAB[:, :, :]).then_inc(stored, 16)
                    sp.wait_ge(stored, 16 * NG)

                @block.scalar
                def _(act):
                    with act.Fori(0, NG) as g:
                        act.wait_ge(turned, g + 1)
                        nc.scalar.copy(XT[:, :], PS[0:D, 0:WG * P]).then_inc(xt_ready, 1)

                @block.vector
                def _(dve):
                    nc.vector.tensor_tensor(WE[:, 0:D], Wt[:, W_EDGE_I:W_EDGE_I + D], Wt[:, W_EDGE_J:W_EDGE_J + D],
                                            ALU.subtract).then_inc(we_ready, 1)
                    nc.vector.tensor_copy(WE[:, D:2 * D], Wt[:, W_EDGE_J:W_EDGE_J + D]).then_inc(we_ready, 1)
                    with dve.Fori(0, NG) as g:
                        gl = Chain(dve, gseq, g * 6)
                        w = bass.ds(g * WG, WG)
                        nc.vector.tensor_copy(stage[:, :, :], X3[:, w, :]).then_inc(staged, 1)
                        dve.wait_ge(made, g + 1)
                        nc.vector.tensor_copy(TAB[:, :, :], pq[:, :, D:2 * D]).then_inc(tab_ready, 1)
                        gl(nc.vector.tensor_tensor(full[:, :, :], pq[:, :, 0:D], rows_of(vec(V_EDGE_B), WG), ALU.add))
                        split3(gl, full[:, :, :], part2[:, w, 0, :], part2[:, w, 1, :], part2[:, w, 2, :],
                               rest[:, :, :])
                        dve.wait_ge(stored, g * 16 + 16)

                @block.tensor
                def _(pe):
                    pe.wait_ge(we_ready, 2)
                    with pe.Fori(0, NG) as g:
                        hold(pe, "tensor", staged, g + 1)
                        for j in range(WG):
                            ins = nc.tensor.transpose(PS[0:D, j * P:(j + 1) * P], stage[:, j, :], ident[:, :])
                        ins.then_inc(turned, 1)
                        pe.wait_ge(xt_ready, g + 1)
                        for j in range(WG):
                            ins = nc.tensor.matmul(pq[:, j, :], XT[:, j * P:(j + 1) * P], WE[:, :],
                                                   start=True, stop=True)
                        ins.then_inc(made, 1)

        with Phase("edge_a") as ph:
            G = ph.sb("G", [P, 2, B, D])
            KEYS = ph.sb("KEYS", [P, 2, BE], BF16)
            OHT = ph.sb("OHT", [P, 2, B, P], BF16)
            HS = ph.sb("HS", [P, 2, B, D])
            SQ = ph.sb("SQ", [P, 2, B, D])
            mom = ph.sb("mom", [D, 4])
            momb = ph.sb("momb", [D, 2, P])
            keys_in = [ph.sem(f"keys_in{s}") for s in range(2)]
            rows_in = [ph.sem(f"rows_in{s}") for s in range(2)]
            stored = [ph.sem(f"stored{s}") for s in range(2)]
            idx_ready, oht_ready, dst_done = ph.sem("idx_ready"), ph.sem("oht_ready"), ph.sem("dst_done")
            h_ready, sq_ready, summed = ph.sem("h_ready"), ph.sem("sq_ready"), ph.sem("summed")
            seq, zeroed, spread, spread_ready = ph.sem("seq"), ph.sem("zeroed"), ph.sem("spread"), ph.sem("spread_ready")
            to_root, rooted = ph.sem("to_root"), ph.sem("rooted")
            with nc.Block() as block:
                @block.gpsimd
                def _(pool):
                    gather_rows(pool, edge_table, lambda s, u: G[:, s, u, :], idx_ready, h_ready, rows_in)

                @block.sync
                def _(sp):
                    def turn(t):
                        for s in range(2):
                            b = t * 2 + s
                            ring_free(sp, oht_ready, b)
                            sp.dma_start(KEYS[:, s, :], key_flat.rearrange("k e -> (k e)").unsqueeze(0)
                                         [:, bass.ds(b * BE, BE)].to_broadcast([P, BE])).then_inc(keys_in[s], 16)
                        for s in range(2):
                            b = t * 2 + s
                            sp.wait_ge(h_ready, b + 1)
                            sp.dma_start(held[bass.ds(b * P, P), 0:B * D],
                                         HS[:, s].rearrange("p b d -> p (b d)")).then_inc(stored[s], 16)
                    over_turns(sp, turn)
                    for s in range(2):
                        sp.wait_ge(stored[s], 16 * TURNS)

                @block.scalar
                def _(act):
                    def turn(t):
                        for s in range(2):
                            b = t * 2 + s
                            act.wait_ge(h_ready, b + 1)
                            ring_free(act, summed, b)
                            nc.scalar.activation(SQ[:, s], HS[:, s], ACT.Square).then_inc(sq_ready, 1)
                    over_turns(act, turn)
                    act.wait_ge(to_root, 1)
                    nc.scalar.activation(mom[:, 3:4], mom[:, 2:3], ACT.Sqrt).then_inc(rooted, 1)

                @block.vector
                def _(dve):
                    put_indices(src_idx, 0, 0, idx_ready)
                    put_indices(src_idx, 1, 1, idx_ready)
                    nc.vector.memset(bank(4), 0.0).then_inc(zeroed, 1)

                    def turn(t):
                        for s in range(2):
                            b = t * 2 + s
                            dve.wait_ge(keys_in[s], 16 * (t + 1))
                            ring_free(dve, dst_done, b)
                            nc.vector.tensor_scalar(OHT[:, s].rearrange("p b e -> p (b e)"), KEYS[:, s, :],
                                                    iotaT[:, 0:1], None, ALU.is_equal).then_inc(oht_ready, 1)
                            dve.wait_ge(rows_in[s], P * (t + 1))
                            put_indices(src_idx, b + 2, s, idx_ready)
                            dve.wait_ge(dst_done, b + 1)
                            if not (isinstance(b, int) and b < 2):
                                dve.wait_ge(summed, b - 1)
                                dve.wait_ge(stored[s], 16 * t)
                            nc.vector.tensor_tensor(HS[:, s], bank(s).rearrange("p (b d) -> p b d", d=D),
                                                    G[:, s], ALU.add).then_inc(h_ready, 1)
                    over_turns(dve, turn)
                    dve.wait_ge(summed, BATCHES)
                    link = Chain(dve, seq)
                    link(nc.vector.tensor_scalar(mom[:, 0:2], bank(4)[0:D, 0:2], 1.0 / E, None, ALU.mult))
                    link(nc.vector.tensor_tensor(mom[:, 2:3], mom[:, 0:1], mom[:, 0:1], ALU.mult))
                    link(nc.vector.tensor_tensor(mom[:, 2:3], mom[:, 1:2], mom[:, 2:3], ALU.subtract))
                    link(nc.vector.tensor_scalar(mom[:, 2:3], mom[:, 2:3], 0.0, LN_EPS, ALU.max, ALU.add))
                    nc.vector.tensor_copy(momb[:, 0, :], mom[:, 0:1].to_broadcast([D, P])).then_inc(to_root, 1)
                    dve.wait_ge(rooted, 1)
                    link(nc.vector.reciprocal(mom[:, 1:2], mom[:, 3:4]))
                    nc.vector.tensor_copy(momb[:, 1, :], mom[:, 1:2].to_broadcast([D, P])).then_inc(spread_ready, 1)
                    dve.wait_ge(spread, 1)
                    scale, shift = stat[:, 0:D], stat[:, D:2 * D]
                    link(nc.vector.tensor_tensor(scale, bank(5)[:, D:2 * D], vec(V_GAMMA), ALU.mult))
                    link(nc.vector.tensor_tensor(shift, bank(5)[:, 0:D], scale, ALU.mult))
                    link(nc.vector.tensor_tensor(shift, vec(V_BETA), shift, ALU.subtract))

                @block.tensor
                def _(pe):
                    pe.wait_ge(zeroed, 1)

                    def turn(t):
                        for s in range(2):
                            b = t * 2 + s
                            at = load_places(pe, w_row, b, WINDOWS - 1)
                            pe.wait_ge(oht_ready, b + 1)
                            ring_free(pe, h_ready, b)
                            for u in range(B):
                                for c in range(3):
                                    ins = nc.tensor.matmul(bank(s)[:, u * D:(u + 1) * D], OHT[:, s, u, :],
                                                           part2_at(at[u], c), start=(c == 0), stop=(c == 2))
                            ins.then_inc(dst_done, 1)
                            if not (isinstance(b, int) and b == 0):
                                sum_moments(b - 1, 1 - s)
                    def sum_moments(b, s):
                        pe.wait_ge(sq_ready, b + 1)
                        for u in range(B):
                            one = valid[:, bass.ds(b * B + u, 1)]
                            for c, t in ((0, HS), (1, SQ)):
                                ins = nc.tensor.matmul(bank(4)[0:D, c:c + 1], t[:, s, u, :], one, start=False,
                                                       stop=True, skip_group_check=True)
                        ins.then_inc(summed, 1)
                    over_turns(pe, turn)
                    sum_moments(BATCHES - 1, 1)
                    pe.wait_ge(spread_ready, 1)
                    for c in range(2):
                        ins = nc.tensor.matmul(bank(5)[:, c * D:(c + 1) * D], momb[:, c, :], ident[0:D, 0:D],
                                               start=True, stop=True)
                    ins.then_inc(spread, 1)

        with Phase("edge_b") as ph:
            HS = ph.sb("HS", [P, 2, B, D])
            MSG = ph.sb("MSG", [P, 2, B, D])
            OH = ph.sb("OH", [P, 2, B, P])
            held_in = [ph.sem(f"held_in{s}") for s in range(2)]
            oh_ready, scaled, msg_ready, agg_done = ph.sem("oh_ready"), ph.sem("scaled"), ph.sem("msg_ready"), ph.sem("agg_done")
            seq, zeroed = ph.sem("seq"), ph.sem("zeroed")
            with nc.Block() as block:
                @block.sync
                def _(sp):
                    def turn(t):
                        for s in range(2):
                            b = t * 2 + s
                            ring_free(sp, msg_ready, b)
                            sp.dma_start(HS[:, s].rearrange("p b d -> p (b d)"),
                                         held[bass.ds(b * P, P), 0:B * D]).then_inc(held_in[s], 16)
                    over_turns(sp, turn)

                @block.scalar
                def _(act):
                    def turn(t):
                        for s in range(2):
                            b = t * 2 + s
                            act.wait_ge(scaled, b + 1)
                            ring_free(act, agg_done, b)
                            nc.scalar.activation(MSG[:, s], HS[:, s], ACT.Relu).then_inc(msg_ready, 1)
                    over_turns(act, turn)

                @block.vector
                def _(dve):
                    nc.vector.memset(PS[:, 0:NG * BANK], 0.0).then_inc(zeroed, 1)

                    def turn(t):
                        for s in range(2):
                            b = t * 2 + s
                            link = Chain(dve, seq, b)
                            dve.wait_ge(held_in[s], 16 * (t + 1))
                            link(nc.vector.tensor_tensor(HS[:, s], HS[:, s], rows_of(stat[:, 0:D], B), ALU.mult))
                            nc.vector.tensor_tensor(HS[:, s], HS[:, s], rows_of(stat[:, D:2 * D], B),
                                                    ALU.add).then_inc(scaled, 1)
                            ring_free(dve, agg_done, b)
                            one_hot_edges(OH, s, b).then_inc(oh_ready, 1)
                    over_turns(dve, turn)

                @block.tensor
                def _(pe):
                    pe.wait_ge(zeroed, 1)

                    def turn(t):
                        for s in range(2):
                            b = t * 2 + s
                            at = load_places(pe, a_row, b, A_MAX)
                            pe.wait_ge(oh_ready, b + 1)
                            pe.wait_ge(msg_ready, b + 1)
                            for u in range(B):
                                ins = add_up(pe, OH, s, u, at[u], MSG[:, s, u, :], D)
                            ins.then_inc(agg_done, 1)
                    over_turns(pe, turn)

        with Phase("node3") as ph:
            Y = ph.sb("Y", [P, WINDOWS * D])
            Y3 = Y[:, :].rearrange("p (w d) -> p w d", d=D)
            inv = ph.sb("inv", [P, WINDOWS])
            tools = norm_tools(ph)
            seq = ph.sem("seq")
            with nc.Block() as block:
                @block.scalar
                def _(act):
                    take_root(act, tools, 1)

                @block.vector
                def _(dve):
                    link = Chain(dve, seq)
                    link(nc.vector.reciprocal(inv[:, :], deg[:, :]))
                    for k in range(NG):
                        ins = nc.vector.tensor_tensor(
                            Y3[:, k * WG:(k + 1) * WG, :], sums_psum[:, k, :, 0:D],
                            inv[:, k * WG:(k + 1) * WG].unsqueeze(2).to_broadcast([P, WG, D]), ALU.mult)
                    link(ins)
                    link(nc.vector.tensor_tensor(Y[:, :], Y[:, :], X[:, :], ALU.add))
                    layer_norm(dve, link, Y[:, :], X[:, :], tools, 1)

        with Phase("tables3") as ph:
            stage = ph.sb("stage", [P, WG, D])
            XT = ph.sb("XT", [D, WG * P])
            TAB = ph.sb("TAB", [P, WG, R, T3])
            full = ph.sb("full", [P, WG, Q3])
            rest = ph.sb("rest", [P, WG, Q3])
            staged, turned, xt_ready, p_made = ph.sem("staged"), ph.sem("turned"), ph.sem("xt_ready"), ph.sem("p_made")
            p_taken, q_made, tab_ready, stored = ph.sem("p_taken"), ph.sem("q_made"), ph.sem("tab_ready"), ph.sem("stored")
            gseq = ph.sem("gseq")
            wide = PS[:, BANK:8 * BANK].rearrange("p (j c) -> p j c", c=BANK)[:, :, 0:Q3]
            with nc.Block() as block:
                @block.sync
                def _(sp):
                    with sp.Fori(0, NG) as g:
                        sp.wait_ge(tab_ready, g * 4 + 4)
                        for r in range(R):
                            sp.dma_start(gate_table[bass.ds(g * (WG * P) + r * NP, WG * P), :]
                                         .rearrange("(j p) f -> p j f", p=P), TAB[:, :, r, :]).then_inc(stored, 16)
                    sp.wait_ge(stored, 16 * R * NG)

                @block.scalar
                def _(act):
                    with act.Fori(0, NG) as g:
                        act.wait_ge(turned, g + 1)
                        nc.scalar.copy(XT[:, :], PS[0:D, 0:WG * P]).then_inc(xt_ready, 1)
                        act.wait_ge(q_made, g + 1)
                        for r in range(R):
                            nc.scalar.copy(TAB[:, :, r, 0:D], stage[:, :, :])
                            nc.scalar.copy(TAB[:, :, r, D:2 * D], wide[:, :, 0:D])
                            nc.scalar.copy(TAB[:, :, r, 2 * D:T3], wide[:, :, (r + 1) * D:(r + 2) * D]) \
                                .then_inc(tab_ready, 1)

                @block.vector
                def _(dve):
                    with dve.Fori(0, NG) as g:
                        gl = Chain(dve, gseq, g * 6)
                        w = bass.ds(g * WG, WG)
                        nc.vector.tensor_copy(stage[:, :, :], X3[:, w, :]).then_inc(staged, 1)
                        dve.wait_ge(p_made, g + 1)
                        gl(nc.vector.tensor_tensor(full[:, :, 0:D], wide[:, :, 0:D], rows_of(vec(V_WA_B), WG), ALU.add))
                        nc.vector.tensor_copy(full[:, :, D:Q3], wide[:, :, D:Q3]).then_inc(p_taken, 1)
                        dve.wait_ge(p_taken, g + 1)
                        split3(gl, full[:, :, :], part3[:, w, 0, :], part3[:, w, 1, :], part3[:, w, 2, :],
                               rest[:, :, :])
                        dve.wait_ge(stored, g * (16 * R) + 16 * R)

                @block.tensor
                def _(pe):
                    with pe.Fori(0, NG) as g:
                        hold(pe, "tensor", staged, g + 1)
                        for j in range(WG):
                            ins = nc.tensor.transpose(PS[0:D, j * P:(j + 1) * P], stage[:, j, :], ident[:, :])
                        ins.then_inc(turned, 1)
                        pe.wait_ge(xt_ready, g + 1)
                        for j in range(WG):
                            ins = nc.tensor.matmul(wide[:, j, :], XT[:, j * P:(j + 1) * P],
                                                   Wt[:, W_DST3:W_DST3 + Q3], start=True, stop=True)
                        ins.then_inc(p_made, 1)
                        pe.wait_ge(p_taken, g + 1)
                        for j in range(WG):
                            ins = nc.tensor.matmul(wide[:, j, :], XT[:, j * P:(j + 1) * P],
                                                   Wt[:, W_SRC3:W_SRC3 + Q3], start=True, stop=True)
                        ins.then_inc(q_made, 1)

        with Phase("gate_a") as ph:
            G = ph.sb("G", [P, 2, B, T3])
            CODES = ph.sb("CODES", [P, 2, BE], F16)
            OHT = ph.sb("OHT", [P, 2, R, BE], BF16)
            Z = ph.sb("Z", [P, 2, B, 2 * D])
            L = ph.sb("L", [P, 2, B, D])
            HS = ph.sb("HS", [P, 2, B, AGG])
            keys_in = [ph.sem(f"keys_in{s}") for s in range(2)]
            rows_in = [ph.sem(f"rows_in{s}") for s in range(2)]
            stored = [ph.sem(f"stored{s}") for s in range(2)]
            idx_ready, oht_ready, dst_done = ph.sem("idx_ready"), ph.sem("oht_ready"), ph.sem("dst_done")
            z_ready, gate_ready, rows_used, h_ready = ph.sem("z_ready"), ph.sem("gate_ready"), ph.sem("rows_used"), ph.sem("h_ready")
            seq, ones_in = ph.sem("seq"), ph.sem("ones_in")
            with nc.Block() as block:
                @block.gpsimd
                def _(pool):
                    gather_rows(pool, gate_table, lambda s, u: G[:, s, u, :], idx_ready, h_ready, rows_in)

                @block.sync
                def _(sp):
                    def turn(t):
                        for s in range(2):
                            b = t * 2 + s
                            ring_free(sp, oht_ready, b)
                            sp.dma_start(CODES[:, s, :], code_flat.rearrange("k e -> (k e)").unsqueeze(0)
                                         [:, bass.ds(b * BE, BE)].to_broadcast([P, BE])).then_inc(keys_in[s], 16)
                        for s in range(2):
                            b = t * 2 + s
                            sp.wait_ge(h_ready, b + 1)
                            sp.dma_start(held[bass.ds(b * P, P), :],
                                         HS[:, s].rearrange("p b d -> p (b d)")).then_inc(stored[s], 16)
                    over_turns(sp, turn)
                    for s in range(2):
                        sp.wait_ge(stored[s], 16 * TURNS)

                @block.scalar
                def _(act):
                    def turn(t):
                        for s in range(2):
                            b = t * 2 + s
                            act.wait_ge(z_ready, b + 1)
                            nc.scalar.activation(Z[:, s, :, D:2 * D], Z[:, s, :, D:2 * D],
                                                 ACT.Sigmoid).then_inc(gate_ready, 1)
                    over_turns(act, turn)

                @block.vector
                def _(dve):
                    put_indices(row_idx, 0, 0, idx_ready)
                    put_indices(row_idx, 1, 1, idx_ready)
                    nc.vector.memset(HS[:, :, :, D:AGG], 1.0).then_inc(ones_in, 1)
                    dve.wait_ge(ones_in, 1)

                    def turn(t):
                        for s in range(2):
                            b = t * 2 + s
                            link = Chain(dve, seq, b * 3)
                            dve.wait_ge(keys_in[s], 16 * (t + 1))
                            ring_free(dve, dst_done, b)
                            for r in range(R):
                                ins = nc.vector.tensor_scalar(OHT[:, s, r, :], CODES[:, s, :], iotaT[:, r:r + 1],
                                                              None, ALU.is_equal)
                            ins.then_inc(oht_ready, 1)
                            dve.wait_ge(rows_in[s], P * (t + 1))
                            put_indices(row_idx, b + 2, s, idx_ready)
                            dve.wait_ge(dst_done, b + 1)
                            nc.vector.tensor_tensor(Z[:, s], bank(2 * s, 2).rearrange("p (b f) -> p b f", f=2 * D),
                                                    G[:, s, :, D:T3], ALU.add).then_inc(z_ready, 1)
                            dve.wait_ge(z_ready, b + 1)
                            za = Z[:, s, :, 0:D]
                            link(nc.vector.scalar_tensor_tensor(L[:, s], za, 0.01, za, ALU.mult, ALU.max))
                            link(nc.vector.tensor_tensor(L[:, s], L[:, s], rows_of(vec(V_A3), B), ALU.mult))
                            link(nc.vector.reduce_sum(score[:, bass.ds(b * B, B)], L[:, s], AX_X))
                            dve.wait_ge(gate_ready, b + 1)
                            if not (isinstance(b, int) and b < 2):
                                dve.wait_ge(stored[s], 16 * t)
                            nc.vector.tensor_tensor(HS[:, s, :, 0:D], Z[:, s, :, D:2 * D], G[:, s, :, 0:D],
                                                    ALU.mult).then_inc(h_ready, 1)
                    over_turns(dve, turn)

                @block.tensor
                def _(pe):
                    def turn(t):
                        for s in range(2):
                            b = t * 2 + s
                            at = load_places(pe, w_row, b, WINDOWS - 1)
                            pe.wait_ge(oht_ready, b + 1)
                            ring_free(pe, z_ready, b)
                            for u in range(B):
                                to = bank(2 * s + u // 4)[:, u % 4 * 2 * D:(u % 4 + 1) * 2 * D]
                                for c in range(3):
                                    mine = parts[:, bass.ds(at[u] * (3 * Q3) + c * Q3, Q3)] \
                                        .rearrange("p (k d) -> p k d", d=D)
                                    for r in range(R):
                                        ins = nc.tensor.matmul(
                                            to.rearrange("p (k d) -> p k d", d=D), OHT[:, s, r, u * P:(u + 1) * P],
                                            mine[:, 0:r + 2:r + 1, :], start=(c == 0 and r == 0),
                                            stop=(c == 2 and r == R - 1))
                            ins.then_inc(dst_done, 1)
                    over_turns(pe, turn)

        with Phase("softmax") as ph:
            SR = ph.sb("SR", [P, GROUPS, P])
            S = ph.sb("S", [P, KP])
            K = ph.sb("K", [P, KP])
            K16 = ph.sb("K16", [P, KP], BF16)
            gap = ph.sb("gap", [P, KP + 1])
            fwd = ph.sb("fwd", [P, KP])
            bwd = ph.sb("bwd", [P, KP])
            cols = ph.sb("cols", [P, 8])
            rows = ph.sb("rows", [1, 12, P])
            seq, turned, sr_ready, stored = ph.sem("seq"), ph.sem("turned"), ph.sem("sr_ready"), ph.sem("stored")
            loaded, cols_ready, rows_made = ph.sem("loaded"), ph.sem("cols_ready"), ph.sem("rows_made")
            carry_ready, carry_made, diff_ready = ph.sem("carry_ready"), ph.sem("carry_made"), ph.sem("diff_ready")
            exp_ready, stored2, loaded2, back = ph.sem("exp_ready"), ph.sem("stored2"), ph.sem("loaded2"), ph.sem("back")
            with nc.Block() as block:
                @block.sync
                def _(sp):
                    sp.dma_start(K16[:, :], key_flat.rearrange("(p j) e -> p (j e)", p=P)).then_inc(loaded, 16)
                    sp.wait_ge(sr_ready, 1)
                    sp.dma_start(score_flat.rearrange("(g p) e -> p g e", p=P), SR[:, :, :]).then_inc(stored, 16)
                    sp.wait_ge(stored, 16)
                    sp.dma_start(S[:, :], score_flat.rearrange("(p j) e -> p (j e)", p=P)).then_inc(loaded, 16)
                    sp.wait_ge(exp_ready, 1)
                    sp.dma_start(weight_flat.rearrange("(p j) e -> p (j e)", p=P), S[:, :]).then_inc(stored2, 16)
                    sp.wait_ge(stored2, 16)
                    sp.dma_start(SR[:, :, :], weight_flat.rearrange("(g p) e -> p g e", p=P)).then_inc(loaded2, 16)
                    sp.wait_ge(loaded2, 16)

                @block.scalar
                def _(act):
                    act.wait_ge(turned, 1)
                    nc.scalar.copy(SR[:, :, :].rearrange("p g e -> p (g e)"), PS[:, 0:KP]).then_inc(sr_ready, 1)
                    act.wait_ge(diff_ready, 1)
                    nc.scalar.activation(S[:, :], S[:, :], ACT.Exp).then_inc(exp_ready, 1)
                    act.wait_ge(back, 1)
                    nc.scalar.copy(score[:, :], PS[:, 0:KP])

                @block.tensor
                def _(pe):
                    for g in range(GROUPS):
                        ins = nc.tensor.transpose(PS[:, g * P:(g + 1) * P], score[:, g * P:(g + 1) * P], ident[:, :])
                    ins.then_inc(turned, 1)
                    pe.wait_ge(cols_ready, 1)
                    for c in range(5):
                        ins = nc.tensor.matmul(bank(4 + c // 4)[0:1, c % 4 * P:(c % 4 + 1) * P], cols[:, c:c + 1],
                                               ident[:, :], start=True, stop=True)
                    ins.then_inc(rows_made, 1)
                    pe.wait_ge(carry_ready, 1)
                    for c in range(2):
                        ins = nc.tensor.matmul(bank(6)[:, c:c + 1], rows[:, 10 + c, :], ident[0:1, 0:1],
                                               start=True, stop=True)
                    ins.then_inc(carry_made, 1)
                    pe.wait_ge(loaded2, 16)
                    for g in range(GROUPS):
                        ins = nc.tensor.transpose(PS[:, g * P:(g + 1) * P], SR[:, g, :], ident[:, :])
                    ins.then_inc(back, 1)

                @block.vector
                def _(dve):
                    link = Chain(dve, seq)
                    KN = KP
                    dve.wait_ge(loaded, 32)
                    link(nc.vector.tensor_copy(K[:, :], K16[:, :]))
                    link(nc.vector.memset(gap[:, :], 0.0))
                    link(nc.vector.tensor_tensor(gap[:, 1:KN], K[:, 1:KN], K[:, 0:KN - 1], ALU.not_equal))
                    link(nc.vector.tensor_scalar(gap[:, :], gap[:, :], BIG_NEG, None, ALU.mult))
                    def scan_left(initial):
                        return nc.vector.tensor_tensor_scan(fwd[:, :], gap[:, 0:KN], S[:, :], initial,
                                                            ALU.add, ALU.max)
                    def scan_right(initial):
                        return nc.vector.tensor_tensor_scan(bwd[:, ::-1], gap[:, KN:0:-1], S[:, ::-1], initial,
                                                            ALU.add, ALU.max)
                    link(scan_left(BIG_NEG))
                    link(scan_right(BIG_NEG))
                    link(nc.vector.tensor_copy(cols[:, 0:1], K[:, 0:1]))
                    link(nc.vector.tensor_copy(cols[:, 1:2], K[:, KN - 1:KN]))
                    link(nc.vector.tensor_copy(cols[:, 2:3], fwd[:, KN - 1:KN]))
                    link(nc.vector.tensor_copy(cols[:, 3:4], bwd[:, 0:1]))
                    link(nc.vector.tensor_reduce(cols[:, 4:5], gap[:, 0:KN], AX_X, ALU.min))
                    nc.vector.tensor_copy(cols[:, 5:6], cols[:, 4:5]).then_inc(cols_ready, 1)
                    dve.wait_ge(rows_made, 1)
                    for c in range(5):
                        ins = nc.vector.tensor_copy(rows[:, c, :], bank(4 + c // 4)[0:1, c % 4 * P:(c % 4 + 1) * P])
                    link(ins)
                    first, final, left, right, inner = (rows[:, c, :] for c in range(5))
                    edge, sl, sr, tl, tr = (rows[:, c, :] for c in range(5, 10))
                    into_l, into_r = rows[:, 10, :], rows[:, 11, :]
                    link(nc.vector.memset(rows[:, 5:12, :], BIG_NEG))
                    link(nc.vector.tensor_tensor(edge[:, 1:P], first[:, 1:P], final[:, 0:P - 1], ALU.not_equal))
                    link(nc.vector.tensor_scalar(edge[:, 1:P], edge[:, 1:P], BIG_NEG, None, ALU.mult))
                    link(nc.vector.tensor_tensor(tl, edge, inner, ALU.add))
                    link(nc.vector.tensor_tensor_scan(sl, tl, left, BIG_NEG, ALU.add, ALU.max))
                    link(nc.vector.tensor_tensor(into_l[:, 1:P], sl[:, 0:P - 1], edge[:, 1:P], ALU.add))
                    link(nc.vector.tensor_tensor(tr[:, 0:P - 1], edge[:, 1:P], inner[:, 0:P - 1], ALU.add))
                    link(nc.vector.tensor_tensor_scan(sr[:, ::-1], tr[:, ::-1], right[:, ::-1], BIG_NEG,
                                                      ALU.add, ALU.max))
                    nc.vector.tensor_tensor(into_r[:, 0:P - 1], sr[:, 1:P], edge[:, 1:P],
                                            ALU.add).then_inc(carry_ready, 1)
                    dve.wait_ge(carry_made, 1)
                    link(nc.vector.tensor_copy(cols[:, 6:8], bank(6)[:, 0:2]))
                    link(scan_left(cols[:, 6:7]))
                    link(scan_right(cols[:, 7:8]))
                    link(nc.vector.tensor_tensor(fwd[:, :], fwd[:, :], bwd[:, :], ALU.max))
                    nc.vector.tensor_tensor(S[:, :], S[:, :], fwd[:, :], ALU.subtract).then_inc(diff_ready, 1)

        with Phase("gate_b") as ph:
            HS = ph.sb("HS", [P, 2, B, AGG])
            MSG = ph.sb("MSG", [P, 2, B, AGG])
            OH = ph.sb("OH", [P, 2, B, P])
            held_in = [ph.sem(f"held_in{s}") for s in range(2)]
            oh_ready, msg_ready, agg_done, zeroed = ph.sem("oh_ready"), ph.sem("msg_ready"), ph.sem("agg_done"), ph.sem("zeroed")
            with nc.Block() as block:
                @block.sync
                def _(sp):
                    def turn(t):
                        for s in range(2):
                            b = t * 2 + s
                            ring_free(sp, msg_ready, b)
                            sp.dma_start(HS[:, s].rearrange("p b d -> p (b d)"),
                                         held[bass.ds(b * P, P), :]).then_inc(held_in[s], 16)
                    over_turns(sp, turn)

                @block.vector
                def _(dve):
                    nc.vector.memset(PS[:, 0:NG * BANK], 0.0).then_inc(zeroed, 1)

                    def turn(t):
                        for s in range(2):
                            b = t * 2 + s
                            ring_free(dve, agg_done, b)
                            one_hot_edges(OH, s, b).then_inc(oh_ready, 1)
                            dve.wait_ge(held_in[s], 16 * (t + 1))
                            nc.vector.tensor_tensor(
                                MSG[:, s], HS[:, s],
                                score[:, bass.ds(b * B, B)].unsqueeze(2).to_broadcast([P, B, AGG]),
                                ALU.mult).then_inc(msg_ready, 1)
                    over_turns(dve, turn)

                @block.tensor
                def _(pe):
                    pe.wait_ge(zeroed, 1)

                    def turn(t):
                        for s in range(2):
                            b = t * 2 + s
                            at = load_places(pe, a_row, b, A_MAX)
                            pe.wait_ge(oh_ready, b + 1)
                            pe.wait_ge(msg_ready, b + 1)
                            for u in range(B):
                                ins = add_up(pe, OH, s, u, at[u], MSG[:, s, u, :], AGG)
                            ins.then_inc(agg_done, 1)
                    over_turns(pe, turn)

        with Phase("node4") as ph:
            Y = ph.sb("Y", [P, WINDOWS * D])
            Y3 = Y[:, :].rearrange("p (w d) -> p w d", d=D)
            inv = ph.sb("inv", [P, WINDOWS])
            cat = parts[:, 0:WINDOWS * 4 * D].bitcast(F32).rearrange("p (w f) -> p w f", f=2 * D)
            stage = ph.sb("stage", [P, WG, 2 * D])
            XT = ph.sb("XT", [P, WG * P])
            tools = norm_tools(ph)
            seq, staged, turned, xt_ready = ph.sem("seq"), ph.sem("staged"), ph.sem("turned"), ph.sem("xt_ready")
            made, gseq, x_ready, stored = ph.sem("made"), ph.sem("gseq"), ph.sem("x_ready"), ph.sem("stored")
            with nc.Block() as block:
                @block.sync
                def _(sp):
                    sp.wait_ge(x_ready, 1)
                    full = N // P
                    sp.dma_start(out[0:full * P, :].rearrange("(w p) d -> p w d", p=P),
                                 Y3[:, 0:full, :]).then_inc(stored, 16)
                    sp.dma_start(out[full * P:N, :], Y3[0:N - full * P, full, :]).then_inc(stored, 16)
                    sp.wait_ge(stored, 32)

                @block.scalar
                def _(act):
                    with act.Fori(0, NG) as g:
                        act.wait_ge(turned, g + 1)
                        nc.scalar.copy(XT[:, :], PS[:, 0:WG * P]).then_inc(xt_ready, 1)
                    take_root(act, tools, 1)

                @block.vector
                def _(dve):
                    link = Chain(dve, seq)
                    link(nc.vector.tensor_copy(inv[:, :].rearrange("p (k j) -> p k j", j=WG), sums_psum[:, :, :, D]))
                    link(nc.vector.tensor_scalar(inv[:, :], inv[:, :], 0.5, None, ALU.max))
                    link(nc.vector.reciprocal(inv[:, :], inv[:, :]))
                    for k in range(NG):
                        nc.vector.tensor_tensor(
                            cat[:, k * WG:(k + 1) * WG, D:2 * D], sums_psum[:, k, :, 0:D],
                            inv[:, k * WG:(k + 1) * WG].unsqueeze(2).to_broadcast([P, WG, D]), ALU.mult)
                    link(nc.vector.tensor_copy(cat[:, :, 0:D], X3))
                    with dve.Fori(0, NG) as g:
                        w = bass.ds(g * WG, WG)
                        nc.vector.tensor_copy(stage[:, :, :], cat[:, w, :]).then_inc(staged, 1)
                        dve.wait_ge(made, g + 1)
                        nc.vector.tensor_tensor(Y3[:, w, :], bank(2)[:, 0:WG * D].rearrange("p (j d) -> p j d", d=D),
                                                rows_of(vec(V_LIN3_B), WG), ALU.add).then_inc(gseq, 1)
                    dve.wait_ge(gseq, NG)
                    link(nc.vector.scalar_tensor_tensor(Y[:, :], Y[:, :], 0.01, Y[:, :], ALU.mult, ALU.max))
                    link(nc.vector.tensor_tensor(Y[:, :], Y[:, :], X[:, :], ALU.add))
                    layer_norm(dve, link, Y[:, :], Y[:, :], tools, 1)
                    nc.vector.tensor_copy(X[:, 0:1], Y[:, 0:1]).then_inc(x_ready, 1)

                @block.tensor
                def _(pe):
                    with pe.Fori(0, NG) as g:
                        hold(pe, "tensor", staged, g + 1)
                        for j in range(WG):
                            ins = nc.tensor.transpose(PS[:, j * P:(j + 1) * P], stage[:, j, :], ident[:, :])
                        ins.then_inc(turned, 1)
                        pe.wait_ge(xt_ready, g + 1)
                        for j in range(WG):
                            ins = nc.tensor.matmul(bank(2)[:, j * D:(j + 1) * D], XT[:, j * P:(j + 1) * P], L3[:, :],
                                                   start=True, stop=True)
                        ins.then_inc(made, 1)


def kernel(x, src, dst, edge_type_4, L1_gnn_lin_w, L1_gnn_attn_src, L1_gnn_attn_dst, L1_gnn_out_w, L1_gnn_out_b,
           L1_gnn_ln_g, L1_gnn_ln_b, L2_gnn_W, L2_gnn_b, L2_gnn_gamma, L2_gnn_beta, L3_gnn_r, L3_gnn_a,
           L3_gnn_Wa_w, L3_gnn_Wa_b, L3_gnn_lin_w, L3_gnn_lin_b):
    import concourse.bacc as bacc
    from concourse.bass_utils import run_bass_kernel_spmd

    def tiles(a, pad):
        a = np.asarray(a)
        return np.concatenate([a, np.full(KP * P - E, pad, a.dtype)]).reshape(KP, P)

    edges = np.concatenate([tiles(src, 0), tiles(dst, FAR), tiles(edge_type_4, 0)], axis=1)
    x_pad = np.concatenate([np.asarray(x), np.zeros((NP - N, D), np.float32)])
    lin_w = np.asarray(L1_gnn_lin_w).reshape(H, D, D).transpose(1, 0, 2).reshape(D, H * D)
    out_w = np.asarray(L1_gnn_out_w).reshape(D, H, D).transpose(2, 1, 0).reshape(D, H * D)
    r3 = np.asarray(L3_gnn_r).transpose(1, 0, 2).reshape(2 * D, R * D)
    wa = np.asarray(L3_gnn_Wa_w).T
    edge_w = np.asarray(L2_gnn_W).T
    weights = np.concatenate([
        lin_w, out_w, np.asarray(L1_gnn_attn_src).T, np.asarray(L1_gnn_attn_dst).T,
        edge_w[:D], edge_w[D:], wa[:D], r3[:D], wa[D:], r3[D:]], axis=1)
    vectors = np.concatenate([np.asarray(v).reshape(-1) for v in (
        L1_gnn_out_b, L1_gnn_ln_g, L1_gnn_ln_b, L2_gnn_b, L2_gnn_gamma, L2_gnn_beta,
        np.asarray(L3_gnn_a)[0], L3_gnn_Wa_b, L3_gnn_lin_b)]).reshape(1, NVEC * D)
    order_src = tiles(src, NP)
    arrays = {"x_pad": x_pad, "edges": edges, "order_src": order_src, "weights": weights, "vectors": vectors,
              "lin3": np.asarray(L3_gnn_lin_w).T}
    arrays = {n: np.ascontiguousarray(a) for n, a in arrays.items()}

    nc = bacc.Bacc("TRN2", target_bir_lowering=False, num_devices=1)
    args = [nc.dram_tensor(n, a.shape, mybir.dt.from_np(a.dtype), kind="ExternalInput").ap()
            for n, a in arrays.items()]
    out = nc.dram_tensor("out", (N, D), F32, kind="ExternalOutput").ap()
    build(nc, *args, out)
    result = run_bass_kernel_spmd(nc, [arrays], core_ids=[0])
    return result.results[0]["out"]
```

```python
from contextlib import ExitStack

import numpy as np

import concourse.bass as bass
from concourse import mybir

F32 = mybir.dt.float32
BF16 = mybir.dt.bfloat16
F16 = mybir.dt.float16
I32 = mybir.dt.int32
U32 = mybir.dt.uint32
ALU = mybir.AluOpType
ACT = mybir.ActivationFunctionType
AX_X = mybir.AxisListType.X

P = 128
N = 6250
E = 200000
D = 64
H = 4
R = 4
WINDOWS = -(-N // P)
NP = WINDOWS * P
TILES = -(-E // P)
PAIRS = TILES + WINDOWS - 1
B = 8
BATCHES = 2 * (-(-PAIRS // (2 * B)))
TURNS = BATCHES // 2
GROUPS = -(-(BATCHES * B + 2 * B) // P)
KP = GROUPS * P
BE = B * P
FAR = 1 << 20
LN_EPS = 1e-5
ALPHA_EPS = 1e-9
WG = 7
NG = WINDOWS // WG
BANK = 512
AGG = D + 1
HA = H * D + H
T3 = 3 * D
Q3 = (1 + R) * D
BIG_NEG = -1.0e30
OW = WINDOWS + 1
O_TURNS = -(-TILES // (2 * B))
OT = O_TURNS * 2 * B

W_LIN1 = 0
W_OUT1 = W_LIN1 + H * D
W_ATT = W_OUT1 + H * D
W_EDGE_I = W_ATT + 2 * H
W_EDGE_J = W_EDGE_I + D
W_DST3 = W_EDGE_J + D
W_SRC3 = W_DST3 + Q3
W_COLS = W_SRC3 + Q3
V_OUT_B, V_LN_G, V_LN_B, V_EDGE_B, V_GAMMA, V_BETA, V_A3, V_WA_B, V_LIN3_B = range(9)
NVEC = 9

assert (BATCHES - 6) % 4 == 0
assert OW % 2 == 0 and B * OW <= BANK and OT <= KP and KP - OT <= P
assert WINDOWS % WG == 0 and WG * AGG <= BANK
assert all((w * 37) >> 8 == w // WG for w in range(WINDOWS))


class Chain:

    def __init__(self, eng, sem, base=0):
        self.eng, self.sem, self.base, self.n = eng, sem, base, 0

    def __call__(self, ins):
        self.n += 1
        ins.then_inc(self.sem, 1)
        self.eng.wait_ge(self.sem, self.base + self.n)


def over_turns(eng, body):
    body(0)
    with eng.Fori(1, TURNS) as t:
        body(t)


def over_quads(eng, body):
    for b in range(6):
        body(b, b % 4, b // 4)
    with eng.Fori(0, (BATCHES - 6) // 4) as t:
        for i in range(4):
            body(t * 4 + (6 + i), (6 + i) % 4, t + (6 + i) // 4)


def ring_free4(eng, sem, b):
    if not (isinstance(b, int) and b < 4):
        eng.wait_ge(sem, b - 3)


def ring_free(eng, sem, b):
    if not (isinstance(b, int) and b < 2):
        eng.wait_ge(sem, b - 1)


def build(nc, x_in, edges, order_src, weights, vectors, lin3, out):
    outer = ExitStack()
    with outer:
        def keep(name, shape, dt=F32):
            return outer.enter_context(nc.sbuf_tensor(name, shape, dt))

        def dram(name, shape, dt):
            return nc.dram_tensor(name, shape, dt).ap()

        key_flat = dram("key_flat", (KP, P), BF16)
        key_flat1 = dram("key_flat1", (KP, P), BF16)
        by_src = dram("by_src", (KP, 2 * P), I32)
        code_flat = dram("code_flat", (KP, P), F16)
        att_table = dram("att_table", (NP, D + H), F32)
        edge_table = dram("edge_table", (NP, D), F32)
        gate_table = dram("gate_table", (R * NP, T3), F32)
        held = dram("held", (BATCHES * P, B * AGG), F32)
        score_flat = dram("score_flat", (KP, P), F32)
        weight_flat = dram("weight_flat", (KP, P), F32)

        X = keep("X", [P, WINDOWS * D])
        Wt = keep("Wt", [D, W_COLS])
        Vt = keep("Vt", [P, NVEC * D])
        L3 = keep("L3", [P, D])
        ident = keep("ident", [P, P])
        iotaF = keep("iotaF", [P, P])
        kcol = keep("kcol", [P, GROUPS])
        ones = keep("ones", [P, P], BF16)
        before = keep("before", [P, P], BF16)
        iotaT = keep("iotaT", [P, R])
        key = keep("key", [P, KP])
        valid = keep("valid", [P, KP])
        src_idx = keep("src_idx", [P, KP], U32)
        row_idx = keep("row_idx", [P, KP], U32)
        score = keep("score", [P, KP])
        w_row = keep("w_row", [P, KP], I32)
        a_row = keep("a_row", [P, KP], I32)
        deg = keep("deg", [P, WINDOWS])
        stat = keep("stat", [P, 2 * D])
        idx_now = keep("idx_now", [P, 2, B], U32)
        parts = keep("parts", [P, WINDOWS * 3 * Q3], BF16)
        PS = outer.enter_context(nc.psum_tensor("PS", [P, 8 * BANK], F32))

        part3 = parts[:, :].rearrange("p (w c f) -> p w c f", c=3, f=Q3)
        part2 = parts[:, 0:WINDOWS * 3 * D].rearrange("p (w c f) -> p w c f", c=3, f=D)
        sums1 = parts[:, 0:2 * WINDOWS * HA].bitcast(F32)
        part1 = parts[:, 2 * WINDOWS * HA:2 * WINDOWS * HA + WINDOWS * 3 * H] \
            .rearrange("p (w c f) -> p w c f", c=3, f=H)

        X3 = X[:, :].rearrange("p (w d) -> p w d", d=D)
        sums_psum = PS[:, 0:NG * BANK].rearrange("p (k c) -> p k c", c=BANK)[:, :, 0:WG * AGG] \
            .rearrange("p k (j f) -> p k j f", f=AGG)

        def bank(b, n=1):
            return PS[:, b * BANK:(b + n) * BANK]

        def vec(i):
            return Vt[:, i * D:(i + 1) * D]

        def rows_of(t, w):
            return t.unsqueeze(1).to_broadcast([P, w, D])

        paces = {e: outer.enter_context(nc.semaphore(f"pace_{e}")) for e in ("tensor", "gpsimd")}

        scattered = [outer.enter_context(nc.semaphore(f"scattered{s}")) for s in range(2)]
        pair_rows_in = {n: outer.enter_context(nc.semaphore(f"{n}_rows_in")) for n in ("by_dst", "by_src")}

        def hold(eng, which, sem, value):
            eng.wait_ge(sem, value)
            eng.sem_inc(paces[which], 1)

        spent = []

        def clear_spent():
            assert sorted(spent) == list(range(min(spent), max(spent) + 1))
            with nc.Block() as block:
                @block.sync
                def _(sp):
                    sp.sem_clear(range(min(spent), max(spent) + 1))
            spent.clear()

        class Phase:

            def __init__(self, name):
                self.name, self.ctx = name, ExitStack()

            def __enter__(self):
                self.ctx.__enter__()
                return self

            def __exit__(self, *a):
                return self.ctx.__exit__(*a)

            def sb(self, name, shape, dt=F32):
                return self.ctx.enter_context(nc.sbuf_tensor(f"{self.name}_{name}", shape, dt))

            def sem(self, name):
                new = self.ctx.enter_context(nc.semaphore(f"{self.name}_{name}"))
                assert new.num not in spent
                spent.append(new.num)
                return new

        def layer_norm(dve, link, src, dst, ph, tag):
            mean, var, centred, square, to_root, rooted = ph
            s3 = src.rearrange("p (w d) -> p w d", d=D)
            c3 = centred[:, :].rearrange("p (w d) -> p w d", d=D)
            d3 = dst.rearrange("p (w d) -> p w d", d=D)
            link(nc.vector.reduce_sum(mean[:, :], s3, AX_X))
            link(nc.vector.tensor_scalar(mean[:, :], mean[:, :], 1.0 / D, None, ALU.mult))
            link(nc.vector.tensor_tensor(c3, s3, mean[:, :].unsqueeze(2).to_broadcast([P, WINDOWS, D]),
                                         ALU.subtract))
            link(nc.vector.tensor_tensor(square[:, :], centred[:, :], centred[:, :], ALU.mult))
            link(nc.vector.reduce_sum(var[:, :], square[:, :].rearrange("p (w d) -> p w d", d=D), AX_X))
            nc.vector.tensor_scalar(var[:, :], var[:, :], 1.0 / D, LN_EPS, ALU.mult,
                                    ALU.add).then_inc(to_root, 1)
            dve.wait_ge(rooted, tag)
            link(nc.vector.reciprocal(var[:, :], var[:, :]))
            link(nc.vector.tensor_tensor(d3, c3, var[:, :].unsqueeze(2).to_broadcast([P, WINDOWS, D]),
                                         ALU.mult))

        def norm_tools(ph):
            return (ph.sb("mean", [P, WINDOWS]), ph.sb("var", [P, WINDOWS]), ph.sb("centred", [P, WINDOWS * D]),
                    ph.sb("square", [P, WINDOWS * D]), ph.sem("to_root"), ph.sem("rooted"))

        def take_root(act, tools, tag):
            _, var, _, _, to_root, rooted = tools
            act.wait_ge(to_root, tag)
            nc.scalar.activation(var[:, :], var[:, :], ACT.Sqrt).then_inc(rooted, 1)

        def split3(link, src, hi, mid, low, rest):
            link(nc.vector.tensor_copy(hi, src))
            link(nc.vector.tensor_tensor(rest, src, hi, ALU.subtract))
            link(nc.vector.tensor_copy(mid, rest))
            link(nc.vector.tensor_tensor(rest, rest, mid, ALU.subtract))
            link(nc.vector.tensor_copy(low, rest))

        def gather_rows(pool, table, ring, idx_ready, ring_used, rows_in):
            def turn(t):
                for s in range(2):
                    b = t * 2 + s
                    ring_free(pool, ring_used, b)
                    hold(pool, "gpsimd", idx_ready, b + 1)
                    for u in range(B):
                        pool.indirect_dma_start(
                            out=ring(s, u), out_offset=None, in_=table,
                            in_offset=bass.IndirectOffsetOnAxis(ap=idx_now[:, s, u:u + 1], axis=0),
                        ).then_inc(rows_in[s], 16)
            over_turns(pool, turn)

        def load_keys(sp, flat, ring, b, s, ring_used, keys_in):
            ring_free(sp, ring_used, b)
            sp.dma_start(ring[:, s, :], flat.rearrange("k e -> (k e)").unsqueeze(0)
                         [:, bass.ds(b * BE, BE)].to_broadcast([P, BE])).then_inc(keys_in[s], 16)

        def part1_at(w, c):
            at = 2 * WINDOWS * HA
            return parts[:, bass.ds(w * (3 * H) + (at + c * H), H)]

        def part2_at(w, c):
            return parts[:, bass.ds(w * (3 * D) + c * D, D)]

        def put_indices(idx, b, s, idx_ready):
            nc.vector.tensor_copy(idx_now[:, s, :], idx[:, bass.ds(b * B, B)]).then_inc(idx_ready, 1)

        def one_hot_edges(OH, s, b, key=key):
            return nc.vector.tensor_tensor(
                OH[:, s], iotaF[:, :].unsqueeze(1).to_broadcast([P, B, P]),
                key[:, bass.ds(b * B, B)].unsqueeze(2).to_broadcast([P, B, P]), ALU.is_equal)

        def lower_parts(pool, T, MSG, hi_ready, rest_ready, mid_ready, msg_ready):
            def low(b, s):
                hold(pool, "gpsimd", mid_ready, b + 1)
                nc.gpsimd.tensor_tensor(MSG[:, s, 2], T[:, s], MSG[:, s, 1], ALU.subtract).then_inc(msg_ready, 1)

            def lower(b, s, n):
                hold(pool, "gpsimd", hi_ready, b + 1)
                nc.gpsimd.tensor_tensor(T[:, s], T[:, s], MSG[:, s, 0], ALU.subtract).then_inc(rest_ready, 1)
                if not (isinstance(b, int) and b == 0):
                    low(b - 1, (s - 1) % 4)
            over_quads(pool, lower)
            low(BATCHES - 1, (BATCHES - 1) % 4)

        place_regs = {}

        def load_places(eng, row, b, bound):
            name = str(eng.engine).split(".")[-1]
            if name not in place_regs:
                place_regs[name] = [eng.alloc_register(f"place_{name}_{u}") for u in range(B)]
            eng.load(place_regs[name], row[0:1, bass.ds(b * B, B)])
            return [eng.snap(r, min_val=0, max_val=bound) for r in place_regs[name]]

        A_MAX = (WINDOWS - 1) * AGG + (WINDOWS - 1) // WG * (BANK - WG * AGG)

        def add_up(pe, OH, s, u, a, rows, width):
            return nc.tensor.matmul(PS[:, bass.ds(a, width)], OH[:, s, u, :], rows, start=False,
                                    stop=True, skip_group_check=True)

        with Phase("start") as ph:
            iotaP = ph.sb("iotaP", [P, 1])
            loaded, consts = ph.sem("loaded"), ph.sem("consts")
            with nc.Block() as block:
                @block.sync
                def _(sp):
                    sp.dma_start(X3, x_in.rearrange("(w p) d -> p w d", p=P)).then_inc(loaded, 16)
                    sp.dma_start(Wt[:, :], weights).then_inc(loaded, 16)
                    sp.dma_start(L3[:, :], lin3).then_inc(loaded, 16)
                    sp.dma_start(Vt[:, :], vectors.to_broadcast([P, NVEC * D])).then_inc(loaded, 16)
                    sp.wait_ge(loaded, 64)

                @block.gpsimd
                def _(pool):
                    def count(t, pattern, mult):
                        pool.iota(t, pattern=pattern, base=0, channel_multiplier=mult,
                                  allow_small_or_imprecise_dtypes=True).then_inc(consts, 1)
                    count(kcol[:, :], [[P, GROUPS]], 1)
                    count(iotaF[:, :], [[1, P]], 0)
                    count(iotaP[:, :], [[0, 1]], 1)
                    count(iotaT[:, :], [[P, R]], 1)

                @block.vector
                def _(dve):
                    nc.vector.memset(ones[:, :], 1.0)
                    dve.wait_ge(consts, 4)
                    nc.vector.tensor_scalar(ident[:, :], iotaF[:, :], iotaP[:, :], None, ALU.is_equal)
                    nc.vector.tensor_scalar(before[:, :], iotaF[:, :], iotaP[:, :], None, ALU.is_gt)

        with Phase("order") as ph:
            raw = ph.sb("raw", [P, 2, GROUPS, P], I32)
            rawf = parts[:, 0:4 * KP].bitcast(F32).rearrange("p (f g e) -> p f g e", f=2, e=P)
            pay = ph.sb("pay", [P, KP, 2], I32)
            win = parts[:, 6 * KP:8 * KP].bitcast(F32)
            wini = parts[:, 4 * KP:6 * KP].bitcast(I32)
            fill = ph.sb("fill", [KP - OT, 2 * P], I32)
            OHW = ph.sb("OHW", [P, 2, B, OW], BF16)
            win16 = ph.sb("win16", [P, KP], BF16)
            IN = ph.sb("IN", [P, 2, KP], BF16)
            ones32 = ph.sb("ones32", [P, P])
            hist, upto, zero = ph.sb("hist", [P, OW]), ph.sb("upto", [P, OW]), ph.sb("zero", [P, OW])
            A = ph.sb("A", [P, 2, B + 1, OW])
            Q = ph.sb("Q", [P, 2, B, OW])
            placef = ph.sb("placef", [P, 2, B])
            pay_now = ph.sb("pay_now", [P, 2, B, 2], I32)
            loaded, rawf_ready, columns, filled = ph.sem("loaded"), ph.sem("rawf_ready"), ph.sem("columns"), ph.sem("filled")
            fill_out, seq, counted = ph.sem("fill_out"), ph.sem("seq"), ph.sem("counted")
            in_window, part_counts, added_up = ph.sem("in_window"), ph.sem("part_counts"), ph.sem("added_up")
            oh2, ranked, q_ready, qseq = ph.sem("oh2"), ph.sem("ranked"), ph.sem("q_ready"), ph.sem("qseq")
            place_ready = ph.sem("place_ready")

            def windows_of(s, b):
                return nc.vector.tensor_tensor(
                    OHW[:, s], iotaF[:, 0:OW].unsqueeze(1).to_broadcast([P, B, OW]),
                    win[:, bass.ds(b * B, B)].unsqueeze(2).to_broadcast([P, B, OW]), ALU.is_equal)

            with nc.Block() as block:
                @block.sync
                def _(sp):
                    sp.dma_start(raw[:, 0], order_src.rearrange("(g p) e -> p g e", p=P)).then_inc(loaded, 16)
                    sp.dma_start(raw[:, 1], edges.rearrange("(g p) c -> p g c", p=P)[:, :, P:2 * P]).then_inc(loaded, 16)
                    sp.wait_ge(filled, 1)
                    sp.dma_start(by_src[OT:KP, :], fill[:, :]).then_inc(fill_out, 16)
                    sp.wait_ge(fill_out, 16)

                @block.gpsimd
                def _(pool):
                    to = by_src.rearrange("t (e f) -> (t e) f", f=2)

                    def turn(t):
                        for s in range(2):
                            b = t * 2 + s
                            hold(pool, "gpsimd", place_ready, b + 1)
                            for u in range(B):
                                pool.indirect_dma_start(
                                    out=to, out_offset=bass.IndirectOffsetOnAxis(ap=idx_now[:, s, u:u + 1], axis=0),
                                    in_=pay_now[:, s, u, :], in_offset=None).then_inc(scattered[s], 16)
                    turn(0)
                    with pool.Fori(1, O_TURNS) as t:
                        turn(t)
                    for s in range(2):
                        pool.wait_ge(scattered[s], P * O_TURNS)

                @block.tensor
                def _(pe):
                    pe.wait_ge(rawf_ready, 1)
                    for f in range(2):
                        for g in range(GROUPS):
                            at = f * 4 * BANK + g * P
                            ins = nc.tensor.transpose(PS[:, at:at + P], rawf[:, f, g, :], ident[:, :])
                    ins.then_inc(columns, 1)

                    def count(t):
                        for s in range(2):
                            w = t * 2 + s
                            hold(pe, "tensor", in_window, w + 1)
                            for g in range(GROUPS):
                                ins = nc.tensor.matmul(PS[:, bass.ds(w + 5 * BANK, 1)], IN[:, s, g * P:(g + 1) * P],
                                                       ones[:, 0:1], start=(g == 0), stop=(g == GROUPS - 1))
                            ins.then_inc(counted, 1)
                    with pe.Fori(0, OW // 2) as t:
                        count(t)
                    pe.wait_ge(part_counts, 1)
                    nc.tensor.matmul(bank(6)[:, 0:OW], ones32[:, :], hist[:, :], start=True,
                                     stop=True).then_inc(added_up, 1)

                    def rank(t):
                        for s in range(2):
                            b = t * 2 + s
                            pe.wait_ge(oh2, b + 1)
                            ring_free(pe, q_ready, b)
                            oh = OHW[:, s].rearrange("p t w -> p (t w)")
                            nc.tensor.matmul(bank(s)[:, 0:B * OW], before[:, :], oh, start=True, stop=True)
                            nc.tensor.matmul(bank(2 + s)[:, 0:B * OW], ones[:, :], oh, start=True,
                                             stop=True).then_inc(ranked, 1)
                    rank(0)
                    with pe.Fori(1, O_TURNS) as t:
                        rank(t)

                @block.vector
                def _(dve):
                    link = Chain(dve, seq)
                    nc.vector.memset(fill[:, :], FAR).then_inc(filled, 1)
                    dve.wait_ge(loaded, 32)
                    nc.vector.tensor_copy(rawf[:, :, :, :], raw[:, :, :, :]).then_inc(rawf_ready, 1)
                    dve.wait_ge(columns, 1)
                    link(nc.vector.tensor_copy(pay[:, :, 0], PS[:, 0:KP]))
                    link(nc.vector.tensor_copy(pay[:, :, 1], PS[:, 4 * BANK:4 * BANK + KP]))
                    link(nc.vector.tensor_scalar(wini[:, :], pay[:, :, 0], 7, None, ALU.arith_shift_right))
                    link(nc.vector.tensor_copy(win[:, :], wini[:, :]))
                    link(nc.vector.tensor_copy(win16[:, :], wini[:, :]))
                    nc.vector.memset(ones32[:, :], 1.0)

                    def count(t):
                        for s in range(2):
                            w = t * 2 + s
                            ring_free(dve, counted, w)
                            nc.vector.tensor_scalar(IN[:, s, :], win16[:, :], iotaF[:, bass.ds(w, 1)], None,
                                                    ALU.is_equal).then_inc(in_window, 1)
                    count(0)
                    with dve.Fori(1, OW // 2) as t:
                        count(t)
                    dve.wait_ge(counted, OW)
                    nc.vector.tensor_copy(hist[:, :], bank(5)[:, 0:OW]).then_inc(part_counts, 1)
                    dve.wait_ge(added_up, 1)
                    link(nc.vector.tensor_copy(hist[:, :], bank(6)[:, 0:OW]))
                    link(nc.vector.memset(zero[:, :], 0.0))
                    link(nc.vector.tensor_tensor_scan(upto[:, :], hist[:, :], zero[:, :], 0.0, ALU.add, ALU.add))
                    link(nc.vector.tensor_tensor(A[:, 1, B, :], upto[:, :], hist[:, :], ALU.subtract))

                    def place(t):
                        for s in range(2):
                            b = t * 2 + s
                            ql = Chain(dve, qseq, b * (B + 4))
                            windows_of(s, b).then_inc(oh2, 1)
                            ql(nc.vector.tensor_copy(A[:, s, 0, :], A[:, 1 - s, B, :]))
                            dve.wait_ge(ranked, b + 1)
                            tot = bank(2 + s)[:, 0:B * OW].rearrange("p (t w) -> p t w", w=OW)
                            for u in range(B):
                                ql(nc.vector.tensor_tensor(A[:, s, u + 1, :], A[:, s, u, :], tot[:, u, :], ALU.add))
                            ql(nc.vector.tensor_tensor(Q[:, s], bank(s)[:, 0:B * OW].rearrange("p (t w) -> p t w", w=OW),
                                                       A[:, s, 0:B, :], ALU.add))
                            nc.vector.tensor_tensor(Q[:, s], Q[:, s], OHW[:, s], ALU.mult).then_inc(q_ready, 1)
                            dve.wait_ge(q_ready, b + 1)
                            ql(nc.vector.reduce_sum(placef[:, s, :], Q[:, s], AX_X))
                            if not (isinstance(b, int) and b < 2):
                                dve.wait_ge(scattered[s], P * t)
                            ql(nc.vector.tensor_copy(idx_now[:, s, :], placef[:, s, :]))
                            nc.vector.tensor_copy(pay_now[:, s], pay[:, bass.ds(b * B, B), :]).then_inc(place_ready, 1)
                    place(0)
                    with dve.Fori(1, O_TURNS) as t:
                        place(t)

        def pair_up(name, table, fields_n, interleaved, key, gather_idx, w_row, key_to, typed):
            ph = Phase(name)
            with ph:
                pair_up_in(ph, table, fields_n, interleaved, key, gather_idx, w_row, key_to, typed)

        def pair_up_in(ph, table, fields_n, interleaved, key, gather_idx, w_row, key_to, typed):
            last = ph.sb("last", [P, GROUPS], I32)
            wl = ph.sb("wl", [P, GROUPS], I32)
            ends = ph.sb("ends", [P, GROUPS])
            past = parts[:, 0:GROUPS * KP].rearrange("p (g k) -> p g k", k=KP)
            iotaK = parts[:, GROUPS * KP:(GROUPS + 2) * KP].bitcast(F32)
            wbc = ph.sb("wbc", [P, KP])
            sev = ph.sb("sev", [P, KP], I32)
            tcol = ph.sb("tcol", [P, GROUPS], U32)
            wcol = ph.sb("wcol", [P, GROUPS])
            rows_i = ph.sb("rows_i", [P, GROUPS, fields_n * P], I32)
            last_in, consts = ph.sem("last_in"), ph.sem("consts")
            seq, past_ready, counted = ph.sem("seq"), ph.sem("past_ready"), ph.sem("counted")
            tiles_ready, rows_in = ph.sem("tiles_ready"), pair_rows_in[ph.name]
            with nc.Block() as block:
                @block.sync
                def _(sp):
                    sp.dma_start(last[:, :].unsqueeze(2),
                                 table.rearrange("(g p) c -> p g c", p=P)[:, :, 2 * P - 2:2 * P - 1] if interleaved
                                 else table.rearrange("(g p) c -> p g c", p=P)[:, :, 2 * P - 1:2 * P],
                                 allow_slow_non_contiguous=True).then_inc(last_in, 16)

                @block.gpsimd
                def _(pool):
                    def count(t, pattern, mult):
                        pool.iota(t, pattern=pattern, base=0, channel_multiplier=mult,
                                  allow_small_or_imprecise_dtypes=True).then_inc(consts, 1)
                    count(iotaK[:, :], [[1, KP]], 0)
                    pool.wait_ge(tiles_ready, 1)
                    for g in range(GROUPS):
                        pool.indirect_dma_start(
                            out=rows_i[:, g, :], out_offset=None, in_=table,
                            in_offset=bass.IndirectOffsetOnAxis(ap=tcol[:, g:g + 1], axis=0)).then_inc(rows_in, 16)
                    pool.wait_ge(rows_in, 16 * GROUPS)

                @block.vector
                def _(dve):
                    link = Chain(dve, seq)
                    nc.vector.memset(score[:, :], 0.0)
                    dve.wait_ge(consts, 1)
                    dve.wait_ge(last_in, 16)
                    link(nc.vector.tensor_scalar(wl[:, :], last[:, :], 7, None, ALU.arith_shift_right))
                    link(nc.vector.tensor_scalar(ends[:, :], wl[:, :], float(WINDOWS - 1), None, ALU.min))
                    link(nc.vector.tensor_tensor(ends[:, :], ends[:, :], kcol[:, :], ALU.add))
                    for g in range(GROUPS):
                        ins = nc.vector.tensor_scalar(past[:, g, :], iotaK[:, :], ends[:, g:g + 1], None, ALU.is_gt)
                    ins.then_inc(past_ready, 1)
                    dve.wait_ge(counted, 1)
                    link(nc.vector.tensor_copy(wcol[:, :], bank(4)[:, 0:GROUPS]))
                    nc.vector.tensor_copy(tcol[:, :], wcol[:, :]).then_inc(tiles_ready, 1)
                    dve.wait_ge(tiles_ready, 1)
                    link(nc.vector.tensor_tensor(wcol[:, :], kcol[:, :], wcol[:, :], ALU.subtract))
                    link(nc.vector.tensor_scalar(wcol[:, :], wcol[:, :], float(WINDOWS - 1), float(P), ALU.min, ALU.mult))
                    c4 = KP // 4
                    for c in range(4):
                        ins = nc.vector.tensor_tensor(wbc[:, c * c4:(c + 1) * c4], iotaK[:, c * c4:(c + 1) * c4],
                                                      bank(c)[:, 0:c4], ALU.subtract)
                    link(ins)
                    link(nc.vector.tensor_scalar(wbc[:, :], wbc[:, :], float(WINDOWS - 1), None, ALU.min))
                    link(nc.vector.tensor_copy(w_row, wbc[:, :]))
                    if typed:
                        link(nc.vector.tensor_scalar(sev[:, :], wbc[:, :], 37.0, None, ALU.mult))
                        link(nc.vector.tensor_scalar(sev[:, :], sev[:, :], 8, None, ALU.arith_shift_right))
                        link(nc.vector.tensor_scalar(a_row[:, :], sev[:, :], float(BANK - WG * AGG), None, ALU.mult))
                        link(nc.vector.scalar_tensor_tensor(a_row[:, :], wbc[:, :], float(AGG), a_row[:, :],
                                                            ALU.mult, ALU.add))
                    link(nc.vector.tensor_scalar(key, wbc[:, :], float(P), None, ALU.mult))

                @block.tensor
                def _(pe):
                    pe.wait_ge(past_ready, 1)
                    c4 = KP // 4
                    for c in range(4):
                        for g in range(GROUPS):
                            nc.tensor.matmul(bank(c)[:, 0:c4], ones[:, :], past[:, g, c * c4:(c + 1) * c4],
                                             start=(g == 0), stop=(g == GROUPS - 1))
                    for j in range(GROUPS):
                        for g in range(GROUPS):
                            ins = nc.tensor.matmul(bank(4)[:, j:j + 1], past[:, g, j * P:(j + 1) * P], ones[:, 0:1],
                                                   start=(g == 0), stop=(g == GROUPS - 1))
                    ins.then_inc(counted, 1)

            spare = parts[:, 0:12 * KP].bitcast(F32).rearrange("p (f g e) -> p f g e", g=GROUPS, e=P)
            fields, key_r, inside, hit = spare[:, 0:3], spare[:, 3], spare[:, 4], spare[:, 5]
            key_b = ph.sb("key_b", [P, GROUPS, P], BF16)
            code_h = ph.sb("code_h", [P, GROUPS, P], F16)
            seq2, fields_ready, rows_done = ph.sem("seq2"), ph.sem("fields_ready"), ph.sem("rows_done")
            columns, taken, stored = ph.sem("columns"), ph.sem("taken"), ph.sem("stored")
            with nc.Block() as block:
                @block.sync
                def _(sp):
                    sp.wait_ge(rows_done, 1 + typed)
                    sp.dma_start(key_to.rearrange("(g p) e -> p g e", p=P), key_b[:, :, :]).then_inc(stored, 16)
                    if typed:
                        sp.dma_start(code_flat.rearrange("(g p) e -> p g e", p=P), code_h[:, :, :]).then_inc(stored, 16)
                    sp.wait_ge(stored, 16 + 16 * typed)

                @block.vector
                def _(dve):
                    link = Chain(dve, seq2)
                    for f in range(fields_n):
                        from_ = rows_i[:, :, :].rearrange("p g (e f) -> p g f e", f=2)[:, :, 1 - f, :] \
                            if interleaved else rows_i[:, :, f * P:(f + 1) * P]
                        ins = nc.vector.tensor_copy(fields[:, f], from_)
                    ins.then_inc(fields_ready, 1)
                    dve.wait_ge(fields_ready, 1)
                    wb = wcol[:, :].unsqueeze(2).to_broadcast([P, GROUPS, P])
                    link(nc.vector.tensor_tensor(key_r[:, :, :], fields[:, 1], wb, ALU.subtract))
                    link(nc.vector.tensor_scalar(key_r[:, :, :], key_r[:, :, :], -1.0, float(P), ALU.max, ALU.min))
                    nc.vector.tensor_copy(key_b[:, :, :], key_r[:, :, :]).then_inc(rows_done, 1)
                    if typed:
                        link(nc.vector.tensor_scalar(inside[:, :, :], key_r[:, :, :], 0.0, None, ALU.is_ge))
                        link(nc.vector.tensor_scalar(hit[:, :, :], key_r[:, :, :], float(P), None, ALU.is_lt))
                        link(nc.vector.tensor_tensor(inside[:, :, :], inside[:, :, :], hit[:, :, :], ALU.mult))
                        link(nc.vector.scalar_tensor_tensor(key_r[:, :, :], fields[:, 2], float(P), key_r[:, :, :],
                                                            ALU.mult, ALU.add))
                        link(nc.vector.scalar_tensor_tensor(key_r[:, :, :], key_r[:, :, :], 1.0, inside[:, :, :],
                                                            ALU.add, ALU.mult))
                        nc.vector.tensor_scalar(code_h[:, :, :], key_r[:, :, :], -1.0, None,
                                                ALU.add).then_inc(rows_done, 1)
                    dve.wait_ge(columns, 1)
                    nc.vector.tensor_scalar(gather_idx, PS[:, 0:KP], float(NP - 1), None, ALU.min).then_inc(taken, 1)
                    dve.wait_ge(columns, 2)
                    link(nc.vector.tensor_tensor(key, PS[:, 4 * BANK:4 * BANK + KP], key, ALU.subtract))
                    link(nc.vector.tensor_scalar(key, key, -1.0, float(P), ALU.max, ALU.min))
                    if typed:
                        link(nc.vector.tensor_scalar(valid[:, :], key, 0.0, None, ALU.is_ge))
                        link(nc.vector.tensor_scalar(wbc[:, :], key, float(P), None, ALU.is_lt))
                        link(nc.vector.tensor_tensor(valid[:, :], valid[:, :], wbc[:, :], ALU.mult))
                        dve.wait_ge(taken, 1)
                        dve.wait_ge(columns, 3)
                        link(nc.vector.scalar_tensor_tensor(row_idx[:, :], PS[:, 0:KP], float(NP), gather_idx,
                                                            ALU.mult, ALU.add))

                @block.tensor
                def _(pe):
                    pe.wait_ge(fields_ready, 1)
                    for f in range(fields_n):
                        if f == 2:
                            pe.wait_ge(taken, 1)
                        for g in range(GROUPS):
                            at = (f % 2) * 4 * BANK + g * P
                            ins = nc.tensor.transpose(PS[:, at:at + P], fields[:, f, g, :], ident[:, :])
                        ins.then_inc(columns, 1)

        by_src_key, by_src_idx, by_src_w = (
            parts[:, WINDOWS * 3 * Q3 - (i + 1) * 2 * KP:WINDOWS * 3 * Q3 - i * 2 * KP].bitcast(dt)
            for i, dt in enumerate((F32, U32, I32)))
        pair_up("by_dst", edges, 3, False, key[:, :], src_idx[:, :], w_row[:, :], key_flat, True)
        pair_up("by_src", by_src, 2, True, by_src_key, by_src_idx, by_src_w, key_flat1, False)
        clear_spent()

        with Phase("mean") as ph:
            G = ph.sb("G", [P, 2, B, AGG])
            OH = ph.sb("OH", [P, 2, B, P])
            idx_ready, oh_ready, agg_done = ph.sem("idx_ready"), ph.sem("oh_ready"), ph.sem("agg_done")
            rows_in = [ph.sem(f"rows_in{s}") for s in range(2)]
            zeroed = ph.sem("zeroed")
            with nc.Block() as block:
                @block.gpsimd
                def _(pool):
                    gather_rows(pool, x_in, lambda s, u: G[:, s, u, 0:D], idx_ready, agg_done, rows_in)

                @block.vector
                def _(dve):
                    put_indices(src_idx, 0, 0, idx_ready)
                    put_indices(src_idx, 1, 1, idx_ready)
                    nc.vector.memset(PS[:, 0:NG * BANK], 0.0).then_inc(zeroed, 1)
                    nc.vector.memset(G[:, :, :, D:AGG], 1.0).then_inc(zeroed, 1)

                    def turn(t):
                        for s in range(2):
                            b = t * 2 + s
                            ring_free(dve, agg_done, b)
                            one_hot_edges(OH, s, b).then_inc(oh_ready, 1)
                            dve.wait_ge(rows_in[s], P * (t + 1))
                            put_indices(src_idx, b + 2, s, idx_ready)
                    over_turns(dve, turn)

                @block.tensor
                def _(pe):
                    pe.wait_ge(zeroed, 2)

                    def turn(t):
                        for s in range(2):
                            b = t * 2 + s
                            at = load_places(pe, a_row, b, A_MAX)
                            pe.wait_ge(oh_ready, b + 1)
                            pe.wait_ge(rows_in[s], P * (t + 1))
                            for u in range(B):
                                ins = add_up(pe, OH, s, u, at[u], G[:, s, u, :], AGG)
                            ins.then_inc(agg_done, 1)
                    over_turns(pe, turn)

        with Phase("node1") as ph:
            Y = ph.sb("Y", [P, WINDOWS * D])
            Y3 = Y[:, :].rearrange("p (w d) -> p w d", d=D)
            inv = ph.sb("inv", [P, WINDOWS])
            WA = ph.sb("WA", [D, 2 * H])
            stage = ph.sb("stage", [P, WG, D])
            XT = ph.sb("XT", [D, WG * P])
            TAB = ph.sb("TAB", [P, WG, D + H])
            rest = ph.sb("rest", [P, WG, H])
            a_dst = ph.sb("a_dst", [P, WG, H])
            tools = norm_tools(ph)
            seq, wa_done, wa_ready = ph.sem("seq"), ph.sem("wa_done"), ph.sem("wa_ready")
            staged = ph.sem("staged")
            turned, xt_ready, made, taken = ph.sem("turned"), ph.sem("xt_ready"), ph.sem("made"), ph.sem("taken")
            gseq, tab_ready, stored = ph.sem("gseq"), ph.sem("tab_ready"), ph.sem("stored")
            with nc.Block() as block:
                @block.scalar
                def _(act):
                    take_root(act, tools, 1)
                    act.wait_ge(wa_ready, 1)
                    with act.Fori(0, NG) as g:
                        nc.scalar.copy(stage[:, :, :], X3[:, bass.ds(g * WG, WG), :]).then_inc(staged, 1)
                        act.wait_ge(turned, g + 1)
                        nc.scalar.copy(XT[:, :], PS[0:D, 0:WG * P]).then_inc(xt_ready, 1)

                @block.vector
                def _(dve):
                    link = Chain(dve, seq)
                    link(nc.vector.tensor_copy(deg[:, :].rearrange("p (k j) -> p k j", j=WG), sums_psum[:, :, :, D]))
                    link(nc.vector.tensor_scalar(deg[:, :], deg[:, :], 1.0, None, ALU.max))
                    link(nc.vector.reciprocal(inv[:, :], deg[:, :]))
                    for k in range(NG):
                        ins = nc.vector.tensor_tensor(
                            Y3[:, k * WG:(k + 1) * WG, :], sums_psum[:, k, :, 0:D],
                            inv[:, k * WG:(k + 1) * WG].unsqueeze(2).to_broadcast([P, WG, D]), ALU.mult)
                    link(ins)
                    link(nc.vector.tensor_tensor(Y[:, :], Y[:, :], X[:, :], ALU.add))
                    layer_norm(dve, link, Y[:, :], X[:, :], tools, 1)
                    nc.vector.memset(sums1[:, :], 0.0)
                    dve.wait_ge(wa_done, 1)
                    nc.vector.tensor_copy(WA[:, :], bank(7)[0:D, 0:2 * H]).then_inc(wa_ready, 1)

                    def group(g):
                        gl = Chain(dve, gseq, g * 5)
                        w = bass.ds(g * WG, WG)
                        if not isinstance(g, int):
                            dve.wait_ge(stored, g * 16)
                        nc.vector.tensor_copy(TAB[:, :, 0:D], X3[:, w, :])
                        dve.wait_ge(made, g + 1)
                        m3 = bank(2)[:, 0:WG * 2 * H].rearrange("p (j f) -> p j f", f=2 * H)
                        nc.vector.tensor_copy(TAB[:, :, D:D + H], m3[:, :, 0:H]).then_inc(tab_ready, 1)
                        nc.vector.tensor_copy(a_dst[:, :, :], m3[:, :, H:2 * H]).then_inc(taken, 1)
                        dve.wait_ge(taken, g + 1)
                        split3(gl, a_dst[:, :, :], part1[:, w, 0, :], part1[:, w, 1, :], part1[:, w, 2, :],
                               rest[:, :, :])
                    group(0)
                    with dve.Fori(1, NG) as g:
                        group(g)

                @block.sync
                def _(sp):
                    with sp.Fori(0, NG) as g:
                        sp.wait_ge(tab_ready, g + 1)
                        sp.dma_start(att_table[bass.ds(g * (WG * P), WG * P), :].rearrange("(j p) f -> p j f", p=P),
                                     TAB[:, :, :]).then_inc(stored, 16)
                    sp.wait_ge(stored, 16 * NG)

                @block.tensor
                def _(pe):
                    for c in range(2 * H):
                        h = c % H
                        ins = nc.tensor.matmul(bank(7)[0:D, c:c + 1],
                                               Wt[:, W_LIN1 + h * D:W_LIN1 + (h + 1) * D],
                                               Wt[:, W_ATT + c:W_ATT + c + 1], start=True, stop=True)
                    ins.then_inc(wa_done, 1)
                    pe.wait_ge(wa_ready, 1)

                    def group(g):
                        hold(pe, "tensor", staged, g + 1)
                        for j in range(WG):
                            ins = nc.tensor.transpose(PS[0:D, j * P:(j + 1) * P], stage[:, j, :], ident[:, :])
                        ins.then_inc(turned, 1)
                        pe.wait_ge(xt_ready, g + 1)
                        if not isinstance(g, int):
                            pe.wait_ge(taken, g)
                        for j in range(WG):
                            ins = nc.tensor.matmul(bank(2)[:, j * 2 * H:(j + 1) * 2 * H], XT[:, j * P:(j + 1) * P],
                                                   WA[:, :], start=True, stop=True)
                        ins.then_inc(made, 1)
                    group(0)
                    with pe.Fori(1, NG) as g:
                        group(g)

        with Phase("attention") as ph:
            G = ph.sb("G", [P, 2, B, D + H])
            OH = ph.sb("OH", [P, 2, B, P])
            KEYS = ph.sb("KEYS", [P, 2, BE], BF16)
            OHT = ph.sb("OHT", [P, 2, B, P], BF16)
            AL = ph.sb("AL", [P, 2, B, H])
            MSG = ph.sb("MSG", [P, 2, B, HA])
            keys_in = [ph.sem(f"keys_in{s}") for s in range(2)]
            rows_in = [ph.sem(f"rows_in{s}") for s in range(2)]
            idx_ready, oh_ready, oht_ready = ph.sem("idx_ready"), ph.sem("oh_ready"), ph.sem("oht_ready")
            dst_done, al_ready, exp_ready = ph.sem("dst_done"), ph.sem("al_ready"), ph.sem("exp_ready")
            msg_ready, agg_done, added, seq = ph.sem("msg_ready"), ph.sem("agg_done"), ph.sem("added"), ph.sem("seq")
            part_ready = ph.sem("part_ready")
            sums_bank = [2 + u % 6 for u in range(B)]
            with nc.Block() as block:
                @block.sync
                def _(sp):
                    load_keys(sp, key_flat1, KEYS, 0, 0, oht_ready, keys_in)

                    def turn(t):
                        for s in range(2):
                            load_keys(sp, key_flat1, KEYS, t * 2 + s + 1, 1 - s, oht_ready, keys_in)
                    over_turns(sp, turn)
                    for s in range(2):
                        sp.wait_ge(keys_in[s], 16 * (TURNS + 1 - s))

                @block.gpsimd
                def _(pool):
                    gather_rows(pool, att_table, lambda s, u: G[:, s, u, :], idx_ready, msg_ready, rows_in)

                @block.scalar
                def _(act):
                    def turn(t):
                        for s in range(2):
                            b = t * 2 + s
                            act.wait_ge(al_ready, b + 1)
                            nc.scalar.activation(MSG[:, s, :, H * D:HA], AL[:, s, :, :],
                                                 ACT.Exp).then_inc(exp_ready, 1)
                    over_turns(act, turn)

                @block.vector
                def _(dve):
                    put_indices(by_src_idx, 0, 0, idx_ready)
                    put_indices(by_src_idx, 1, 1, idx_ready)

                    def take_sums(b, u, places):
                        dve.wait_ge(agg_done, b * B + u + 1)
                        if not (isinstance(b, int) and b * B + u == 0):
                            dve.wait_ge(added, b * B + u)
                        to = sums1[:, bass.ds(places[u] * HA, HA)]
                        nc.vector.tensor_tensor(to, to, bank(sums_bank[u])[:, 0:HA], ALU.add).then_inc(added, 1)

                    def one_hot_half(b, s, half):
                        us = slice(half * B // 2, (half + 1) * B // 2)
                        return nc.vector.tensor_tensor(
                            OH[:, s, us], iotaF[:, :].unsqueeze(1).to_broadcast([P, B // 2, P]),
                            by_src_key[:, bass.ds(b * B + half * (B // 2), B // 2)].unsqueeze(2)
                            .to_broadcast([P, B // 2, P]), ALU.is_equal)

                    def weigh(s, q):
                        us = slice(q * B // 4, (q + 1) * B // 4)
                        return nc.vector.tensor_tensor(
                            MSG[:, s, us, 0:H * D].rearrange("p b (h d) -> p b h d", d=D),
                            G[:, s, us, 0:D].unsqueeze(2).to_broadcast([P, B // 4, H, D]),
                            MSG[:, s, us, H * D:HA].unsqueeze(3).to_broadcast([P, B // 4, H, D]), ALU.mult)

                    def one_hot_nodes(s):
                        nc.vector.tensor_scalar(OHT[:, s].rearrange("p b e -> p (b e)"), KEYS[:, s, :],
                                                iotaT[:, 0:1], None, ALU.is_equal).then_inc(oht_ready, 1)

                    dve.wait_ge(keys_in[0], 16)
                    one_hot_nodes(0)
                    one_hot_edges(OH, 0, 0, by_src_key).then_inc(oh_ready, 1)

                    def turn(t):
                        for s in range(2):
                            b = t * 2 + s
                            first = isinstance(b, int) and b == 0
                            link = Chain(dve, seq, b)
                            dve.wait_ge(rows_in[s], P * (t + 1))
                            put_indices(by_src_idx, b + 2, s, idx_ready)
                            dve.wait_ge(dst_done, b + 1)
                            z = bank(s)[:, 0:B * H].rearrange("p (b h) -> p b h", h=H)
                            link(nc.vector.tensor_tensor(AL[:, s], z, G[:, s, :, D:D + H], ALU.add))
                            nc.vector.scalar_tensor_tensor(AL[:, s], AL[:, s], 0.2, AL[:, s], ALU.mult,
                                                           ALU.max).then_inc(al_ready, 1)
                            dve.wait_ge(keys_in[1 - s], 16 * (t + 1 + s))
                            one_hot_nodes(1 - s)
                            if not first:
                                places = load_places(dve, by_src_w, b - 1, WINDOWS - 1)
                            dve.wait_ge(exp_ready, b + 1)
                            for q in range(4):
                                weigh(s, q).then_inc(msg_ready if q == 3 else part_ready, 1)
                                if not first:
                                    take_sums(b - 1, q + 2, places)
                            if not first:
                                dve.wait_ge(agg_done, b * B)
                            one_hot_half(b + 1, 1 - s, 0)
                            if not first:
                                take_sums(b - 1, 6, places)
                            one_hot_half(b + 1, 1 - s, 1).then_inc(oh_ready, 1)
                            if not first:
                                take_sums(b - 1, 7, places)
                            places = load_places(dve, by_src_w, b, WINDOWS - 1)
                            for u in range(2):
                                take_sums(b, u, places)
                    over_turns(dve, turn)
                    places = load_places(dve, by_src_w, BATCHES - 1, WINDOWS - 1)
                    for u in range(2, B):
                        take_sums(BATCHES - 1, u, places)

                @block.tensor
                def _(pe):
                    def spread(b, s):
                        at = load_places(pe, by_src_w, b, WINDOWS - 1)
                        pe.wait_ge(oht_ready, b + 1)
                        ring_free(pe, al_ready, b)
                        for u in range(B):
                            for c in range(3):
                                ins = nc.tensor.matmul(bank(s)[:, u * H:(u + 1) * H], OHT[:, s, u, :],
                                                       part1_at(at[u], c), start=(c == 0), stop=(c == 2))
                        ins.then_inc(dst_done, 1)

                    def sum_heads(b, s):
                        pe.wait_ge(oh_ready, b + 1)
                        for u in range(B):
                            if u == 6:
                                pe.wait_ge(msg_ready, b + 1)
                            elif u % 2 == 0:
                                pe.wait_ge(part_ready, b * 3 + u // 2 + 1)
                            if u >= 6:
                                pe.wait_ge(added, b * B + u - 5)
                            elif not (isinstance(b, int) and b == 0):
                                pe.wait_ge(added, b * B + u - (1 if u < 2 else 7))
                            nc.tensor.matmul(bank(sums_bank[u])[:, 0:HA], OH[:, s, u, :], MSG[:, s, u, :],
                                             start=True, stop=True).then_inc(agg_done, 1)

                    spread(0, 0)

                    def turn(t):
                        for s in range(2):
                            b = t * 2 + s
                            spread(b + 1, 1 - s)
                            sum_heads(b, s)
                    over_turns(pe, turn)

        with Phase("node2") as ph:
            Y = ph.sb("Y", [P, WINDOWS * D])
            Y3 = Y[:, :].rearrange("p (w d) -> p w d", d=D)
            inv = ph.sb("inv", [P, WINDOWS, H])
            C1 = ph.sb("C1", [D, H, D])
            stage = ph.sb("stage", [P, WG, H, D])
            XT = parts[0:D, WINDOWS * 3 * Q3 - 2 * H * WG * P:].bitcast(F32).rearrange("p (h k) -> p h k", h=H)
            tools = norm_tools(ph)
            seq, c_done, c_ready = ph.sem("seq"), ph.sem("c_done"), ph.sem("c_ready")
            staged, turned, xt_ready = ph.sem("staged"), ph.sem("turned"), ph.sem("xt_ready")
            made, gseq, neg_ready, exp_ready = ph.sem("made"), ph.sem("gseq"), ph.sem("neg_ready"), ph.sem("exp_ready")
            with nc.Block() as block:
                @block.scalar
                def _(act):
                    with act.Fori(0, NG) as g:
                        for h in range(H):
                            act.wait_ge(turned, g * H + (h + 1))
                            nc.scalar.copy(XT[:, h, :], PS[0:D, (h % 3) * 2 * BANK:(h % 3) * 2 * BANK + WG * P]) \
                                .then_inc(xt_ready, 1)
                    act.wait_ge(neg_ready, 1)
                    nc.scalar.activation(tools[3][:, :], tools[3][:, :], ACT.Exp).then_inc(exp_ready, 1)
                    take_root(act, tools, 1)
                    take_root(act, tools, 2)

                @block.vector
                def _(dve):
                    link = Chain(dve, seq)
                    dve.wait_ge(c_done, 1)
                    nc.vector.tensor_copy(C1[:, :, :].rearrange("k h o -> k (h o)"),
                                          bank(7)[0:D, 0:H * D]).then_inc(c_ready, 1)
                    dens = sums1.rearrange("p (w c) -> p w c", c=HA)[:, :, H * D:HA]
                    link(nc.vector.tensor_scalar(inv[:, :, :], dens, ALPHA_EPS, None, ALU.add))
                    link(nc.vector.reciprocal(inv[:, :, :], inv[:, :, :]))
                    s4 = sums1.rearrange("p (w c) -> p w c", c=HA)[:, :, 0:H * D]

                    def share(g):
                        w = bass.ds(g * WG, WG)
                        nc.vector.tensor_tensor(
                            stage[:, :, :, :], s4[:, w, :].rearrange("p w (h d) -> p w h d", d=D),
                            inv[:, w, :].unsqueeze(3).to_broadcast([P, WG, H, D]), ALU.mult).then_inc(staged, 1)

                    def add_bias(g):
                        w = bass.ds(g * WG, WG)
                        dve.wait_ge(made, g + 1)
                        nc.vector.tensor_tensor(Y3[:, w, :], bank(6)[:, 0:WG * D].rearrange("p (j d) -> p j d", d=D),
                                                rows_of(vec(V_OUT_B), WG), ALU.add).then_inc(gseq, 1)
                    share(0)
                    with dve.Fori(1, NG) as g:
                        dve.wait_ge(turned, g * H)
                        share(g)
                        add_bias(g - 1)
                    add_bias(NG - 1)
                    dve.wait_ge(gseq, NG)
                    low = tools[3]
                    nc.vector.tensor_scalar(low[:, :], Y[:, :], 0.0, None, ALU.min).then_inc(neg_ready, 1)
                    dve.wait_ge(exp_ready, 1)
                    link(nc.vector.tensor_scalar(low[:, :], low[:, :], -1.0, None, ALU.add))
                    link(nc.vector.scalar_tensor_tensor(Y[:, :], Y[:, :], 0.0, low[:, :], ALU.max, ALU.add))
                    link(nc.vector.tensor_tensor(Y[:, :], Y[:, :], X[:, :], ALU.add))
                    layer_norm(dve, link, Y[:, :], Y[:, :], tools, 1)
                    link(nc.vector.tensor_tensor(Y3, Y3, rows_of(vec(V_LN_G), WINDOWS), ALU.mult))
                    link(nc.vector.tensor_tensor(Y3, Y3, rows_of(vec(V_LN_B), WINDOWS), ALU.add))
                    link(nc.vector.tensor_tensor(Y[:, :], Y[:, :], X[:, :], ALU.add))
                    layer_norm(dve, link, Y[:, :], X[:, :], tools, 2)

                @block.tensor
                def _(pe):
                    for h in range(H):
                        ins = nc.tensor.matmul(bank(7)[0:D, h * D:(h + 1) * D],
                                               Wt[:, W_LIN1 + h * D:W_LIN1 + (h + 1) * D],
                                               Wt[:, W_OUT1 + h * D:W_OUT1 + (h + 1) * D], start=True, stop=True)
                    ins.then_inc(c_done, 1)
                    pe.wait_ge(c_ready, 1)

                    def group(g):
                        hold(pe, "tensor", staged, g + 1)
                        for h in range(H):
                            if h == 3:
                                hold(pe, "tensor", xt_ready, g * H + 1)
                            for j in range(WG):
                                at = (h % 3) * 2 * BANK + j * P
                                ins = nc.tensor.transpose(PS[0:D, at:at + P], stage[:, j, h, :], ident[:, :])
                            ins.then_inc(turned, 1)
                        pe.wait_ge(xt_ready, g * H + H)
                        if not isinstance(g, int):
                            pe.wait_ge(gseq, g)
                        for j in range(WG):
                            for h in range(H):
                                ins = nc.tensor.matmul(bank(6)[:, j * D:(j + 1) * D], XT[:, h, j * P:(j + 1) * P],
                                                       C1[:, h, :], start=(h == 0), stop=(h == H - 1))
                        ins.then_inc(made, 1)
                    group(0)
                    with pe.Fori(1, NG) as g:
                        group(g)

        with Phase("tables2") as ph:
            WE = ph.sb("WE", [D, 2 * D])
            stage = ph.sb("stage", [P, WG, D])
            XT = ph.sb("XT", [D, WG * P])
            TAB = ph.sb("TAB", [P, WG, D])
            full = ph.sb("full", [P, WG, D])
            rest = ph.sb("rest", [P, WG, D])
            staged = ph.sem("staged")
            we_ready, turned, taken = ph.sem("we_ready"), ph.sem("turned"), ph.sem("taken")
            xt_ready, made, gseq = ph.sem("xt_ready"), ph.sem("made"), ph.sem("gseq")
            tab_ready, stored = ph.sem("tab_ready"), ph.sem("stored")
            pq = PS[:, 2 * BANK:2 * BANK + WG * 2 * D].rearrange("p (j f) -> p j f", f=2 * D)
            with nc.Block() as block:
                @block.sync
                def _(sp):
                    with sp.Fori(0, NG) as g:
                        sp.wait_ge(tab_ready, g + 1)
                        sp.dma_start(edge_table[bass.ds(g * (WG * P), WG * P), :].rearrange("(j p) f -> p j f", p=P),
                                     TAB[:, :, :]).then_inc(stored, 16)
                    sp.wait_ge(stored, 16 * NG)

                @block.scalar
                def _(act):
                    with act.Fori(0, NG) as g:
                        nc.scalar.copy(stage[:, :, :], X3[:, bass.ds(g * WG, WG), :]).then_inc(staged, 1)
                        act.wait_ge(turned, g + 1)
                        nc.scalar.copy(XT[:, :], PS[0:D, 0:WG * P]).then_inc(xt_ready, 1)

                @block.vector
                def _(dve):
                    nc.vector.tensor_tensor(WE[:, 0:D], Wt[:, W_EDGE_I:W_EDGE_I + D], Wt[:, W_EDGE_J:W_EDGE_J + D],
                                            ALU.subtract).then_inc(we_ready, 1)
                    nc.vector.tensor_copy(WE[:, D:2 * D], Wt[:, W_EDGE_J:W_EDGE_J + D]).then_inc(we_ready, 1)

                    def group(g):
                        gl = Chain(dve, gseq, g * 5)
                        w = bass.ds(g * WG, WG)
                        dve.wait_ge(made, g + 1)
                        if not isinstance(g, int):
                            dve.wait_ge(stored, g * 16)
                        nc.vector.tensor_copy(TAB[:, :, :], pq[:, :, D:2 * D]).then_inc(tab_ready, 1)
                        nc.vector.tensor_tensor(full[:, :, :], pq[:, :, 0:D], rows_of(vec(V_EDGE_B), WG),
                                                ALU.add).then_inc(taken, 1)
                        dve.wait_ge(taken, g + 1)
                        split3(gl, full[:, :, :], part2[:, w, 0, :], part2[:, w, 1, :], part2[:, w, 2, :],
                               rest[:, :, :])
                    group(0)
                    with dve.Fori(1, NG) as g:
                        group(g)

                @block.tensor
                def _(pe):
                    pe.wait_ge(we_ready, 2)

                    def group(g):
                        hold(pe, "tensor", staged, g + 1)
                        for j in range(WG):
                            ins = nc.tensor.transpose(PS[0:D, j * P:(j + 1) * P], stage[:, j, :], ident[:, :])
                        ins.then_inc(turned, 1)
                        pe.wait_ge(xt_ready, g + 1)
                        if not isinstance(g, int):
                            pe.wait_ge(taken, g)
                        for j in range(WG):
                            ins = nc.tensor.matmul(pq[:, j, :], XT[:, j * P:(j + 1) * P], WE[:, :],
                                                   start=True, stop=True)
                        ins.then_inc(made, 1)
                    group(0)
                    with pe.Fori(1, NG) as g:
                        group(g)

        with Phase("edge_a") as ph:
            G = ph.sb("G", [P, 2, B, D])
            KEYS = ph.sb("KEYS", [P, 2, BE], BF16)
            OHT = ph.sb("OHT", [P, 2, B, P], BF16)
            HS = ph.sb("HS", [P, 2, B, D])
            SQ = ph.sb("SQ", [P, 2, B, D])
            mom = ph.sb("mom", [D, 4])
            momb = ph.sb("momb", [D, 2, P])
            keys_in = [ph.sem(f"keys_in{s}") for s in range(2)]
            rows_in = [ph.sem(f"rows_in{s}") for s in range(2)]
            stored = [ph.sem(f"stored{s}") for s in range(2)]
            idx_ready, oht_ready, dst_done = ph.sem("idx_ready"), ph.sem("oht_ready"), ph.sem("dst_done")
            h_ready, sq_ready, summed = ph.sem("h_ready"), ph.sem("sq_ready"), ph.sem("summed")
            seq, zeroed, spread, spread_ready = ph.sem("seq"), ph.sem("zeroed"), ph.sem("spread"), ph.sem("spread_ready")
            to_root, rooted = ph.sem("to_root"), ph.sem("rooted")
            with nc.Block() as block:
                @block.gpsimd
                def _(pool):
                    gather_rows(pool, edge_table, lambda s, u: G[:, s, u, :], idx_ready, h_ready, rows_in)

                @block.sync
                def _(sp):
                    def turn(t):
                        for s in range(2):
                            b = t * 2 + s
                            load_keys(sp, key_flat, KEYS, b, s, oht_ready, keys_in)
                        for s in range(2):
                            b = t * 2 + s
                            sp.wait_ge(h_ready, b + 1)
                            sp.dma_start(held[bass.ds(b * P, P), 0:B * D],
                                         HS[:, s].rearrange("p b d -> p (b d)")).then_inc(stored[s], 16)
                    over_turns(sp, turn)
                    for s in range(2):
                        sp.wait_ge(stored[s], 16 * TURNS)

                @block.scalar
                def _(act):
                    def turn(t):
                        for s in range(2):
                            b = t * 2 + s
                            act.wait_ge(h_ready, b + 1)
                            ring_free(act, summed, b)
                            nc.scalar.activation(SQ[:, s], HS[:, s], ACT.Square).then_inc(sq_ready, 1)
                    over_turns(act, turn)
                    act.wait_ge(to_root, 1)
                    nc.scalar.activation(mom[:, 3:4], mom[:, 2:3], ACT.Sqrt).then_inc(rooted, 1)

                @block.vector
                def _(dve):
                    put_indices(src_idx, 0, 0, idx_ready)
                    put_indices(src_idx, 1, 1, idx_ready)
                    nc.vector.memset(bank(4), 0.0).then_inc(zeroed, 1)

                    def turn(t):
                        for s in range(2):
                            b = t * 2 + s
                            dve.wait_ge(keys_in[s], 16 * (t + 1))
                            ring_free(dve, dst_done, b)
                            nc.vector.tensor_scalar(OHT[:, s].rearrange("p b e -> p (b e)"), KEYS[:, s, :],
                                                    iotaT[:, 0:1], None, ALU.is_equal).then_inc(oht_ready, 1)
                            dve.wait_ge(rows_in[s], P * (t + 1))
                            put_indices(src_idx, b + 2, s, idx_ready)
                            dve.wait_ge(dst_done, b + 1)
                            if not (isinstance(b, int) and b < 2):
                                dve.wait_ge(summed, b - 1)
                                dve.wait_ge(stored[s], 16 * t)
                            nc.vector.tensor_tensor(HS[:, s], bank(s).rearrange("p (b d) -> p b d", d=D),
                                                    G[:, s], ALU.add).then_inc(h_ready, 1)
                    over_turns(dve, turn)
                    dve.wait_ge(summed, BATCHES)
                    link = Chain(dve, seq)
                    link(nc.vector.tensor_scalar(mom[:, 0:2], bank(4)[0:D, 0:2], 1.0 / E, None, ALU.mult))
                    link(nc.vector.tensor_tensor(mom[:, 2:3], mom[:, 0:1], mom[:, 0:1], ALU.mult))
                    link(nc.vector.tensor_tensor(mom[:, 2:3], mom[:, 1:2], mom[:, 2:3], ALU.subtract))
                    link(nc.vector.tensor_scalar(mom[:, 2:3], mom[:, 2:3], 0.0, LN_EPS, ALU.max, ALU.add))
                    nc.vector.tensor_copy(momb[:, 0, :], mom[:, 0:1].to_broadcast([D, P])).then_inc(to_root, 1)
                    dve.wait_ge(rooted, 1)
                    link(nc.vector.reciprocal(mom[:, 1:2], mom[:, 3:4]))
                    nc.vector.tensor_copy(momb[:, 1, :], mom[:, 1:2].to_broadcast([D, P])).then_inc(spread_ready, 1)
                    dve.wait_ge(spread, 1)
                    scale, shift = stat[:, 0:D], stat[:, D:2 * D]
                    link(nc.vector.tensor_tensor(scale, bank(5)[:, D:2 * D], vec(V_GAMMA), ALU.mult))
                    link(nc.vector.tensor_tensor(shift, bank(5)[:, 0:D], scale, ALU.mult))
                    link(nc.vector.tensor_tensor(shift, vec(V_BETA), shift, ALU.subtract))

                @block.tensor
                def _(pe):
                    pe.wait_ge(zeroed, 1)

                    def turn(t):
                        for s in range(2):
                            b = t * 2 + s
                            at = load_places(pe, w_row, b, WINDOWS - 1)
                            pe.wait_ge(oht_ready, b + 1)
                            ring_free(pe, h_ready, b)
                            for u in range(B):
                                for c in range(3):
                                    ins = nc.tensor.matmul(bank(s)[:, u * D:(u + 1) * D], OHT[:, s, u, :],
                                                           part2_at(at[u], c), start=(c == 0), stop=(c == 2))
                            ins.then_inc(dst_done, 1)
                            if not (isinstance(b, int) and b == 0):
                                sum_moments(b - 1, 1 - s)
                    def sum_moments(b, s):
                        pe.wait_ge(sq_ready, b + 1)
                        for u in range(B):
                            one = valid[:, bass.ds(b * B + u, 1)]
                            for c, t in ((0, HS), (1, SQ)):
                                ins = nc.tensor.matmul(bank(4)[0:D, c:c + 1], t[:, s, u, :], one, start=False,
                                                       stop=True, skip_group_check=True)
                        ins.then_inc(summed, 1)
                    over_turns(pe, turn)
                    sum_moments(BATCHES - 1, 1)
                    pe.wait_ge(spread_ready, 1)
                    for c in range(2):
                        ins = nc.tensor.matmul(bank(5)[:, c * D:(c + 1) * D], momb[:, c, :], ident[0:D, 0:D],
                                               start=True, stop=True)
                    ins.then_inc(spread, 1)

        with Phase("edge_b") as ph:
            HS = ph.sb("HS", [P, 4, B, D])
            NORMED = ph.sb("NORMED", [P, 4, B, D])
            T = ph.sb("T", [P, 4, B, D])
            MSG = ph.sb("MSG", [P, 4, 3, B, D], BF16)
            OH = ph.sb("OH", [P, 4, B, P], BF16)
            held_in = [ph.sem(f"held_in{s}") for s in range(4)]
            oh_ready, mult, scaled = ph.sem("oh_ready"), ph.sem("mult"), ph.sem("scaled")
            hi_ready, rest_ready, mid_ready = ph.sem("hi_ready"), ph.sem("rest_ready"), ph.sem("mid_ready")
            msg_ready, agg_done, zeroed = ph.sem("msg_ready"), ph.sem("agg_done"), ph.sem("zeroed")
            with nc.Block() as block:
                @block.sync
                def _(sp):
                    def load(b, s, n):
                        ring_free4(sp, mult, b)
                        sp.dma_start(HS[:, s].rearrange("p b d -> p (b d)"),
                                     held[bass.ds(b * P, P), 0:B * D]).then_inc(held_in[s], 16)
                    over_quads(sp, load)

                @block.gpsimd
                def _(pool):
                    lower_parts(pool, T, MSG, hi_ready, rest_ready, mid_ready, msg_ready)

                @block.scalar
                def _(act):
                    def mid(b, s):
                        act.wait_ge(rest_ready, b + 1)
                        nc.scalar.copy(MSG[:, s, 1], T[:, s]).then_inc(mid_ready, 1)

                    def part(b, s, n):
                        act.wait_ge(scaled, b + 1)
                        ring_free4(act, agg_done, b)
                        nc.scalar.activation(T[:, s], NORMED[:, s], ACT.Relu)
                        nc.scalar.activation(MSG[:, s, 0], NORMED[:, s], ACT.Relu).then_inc(hi_ready, 1)
                        if not (isinstance(b, int) and b == 0):
                            mid(b - 1, (s - 1) % 4)
                    over_quads(act, part)
                    mid(BATCHES - 1, (BATCHES - 1) % 4)

                @block.vector
                def _(dve):
                    nc.vector.memset(PS[:, 0:NG * BANK], 0.0).then_inc(zeroed, 1)

                    def norm(b, s, n):
                        dve.wait_ge(held_in[s], 16 * (n + 1))
                        ring_free4(dve, hi_ready, b)
                        nc.vector.tensor_tensor(NORMED[:, s], HS[:, s], rows_of(stat[:, 0:D], B),
                                                ALU.mult).then_inc(mult, 1)
                        ring_free4(dve, agg_done, b)
                        one_hot_edges(OH, s, b).then_inc(oh_ready, 1)
                        dve.wait_ge(mult, b + 1)
                        nc.vector.tensor_tensor(NORMED[:, s], NORMED[:, s], rows_of(stat[:, D:2 * D], B),
                                                ALU.add).then_inc(scaled, 1)
                    over_quads(dve, norm)

                @block.tensor
                def _(pe):
                    pe.wait_ge(zeroed, 1)

                    def add(b, s, n):
                        at = load_places(pe, a_row, b, A_MAX)
                        pe.wait_ge(oh_ready, b + 1)
                        pe.wait_ge(msg_ready, b + 1)
                        for u in range(B):
                            for c in range(3):
                                ins = add_up(pe, OH, s, u, at[u], MSG[:, s, c, u, :], D)
                        ins.then_inc(agg_done, 1)
                    over_quads(pe, add)

        with Phase("node3") as ph:
            Y = ph.sb("Y", [P, WINDOWS * D])
            Y3 = Y[:, :].rearrange("p (w d) -> p w d", d=D)
            inv = ph.sb("inv", [P, WINDOWS])
            tools = norm_tools(ph)
            seq = ph.sem("seq")
            with nc.Block() as block:
                @block.scalar
                def _(act):
                    take_root(act, tools, 1)

                @block.vector
                def _(dve):
                    link = Chain(dve, seq)
                    link(nc.vector.reciprocal(inv[:, :], deg[:, :]))
                    for k in range(NG):
                        ins = nc.vector.tensor_tensor(
                            Y3[:, k * WG:(k + 1) * WG, :], sums_psum[:, k, :, 0:D],
                            inv[:, k * WG:(k + 1) * WG].unsqueeze(2).to_broadcast([P, WG, D]), ALU.mult)
                    link(ins)
                    link(nc.vector.tensor_tensor(Y[:, :], Y[:, :], X[:, :], ALU.add))
                    layer_norm(dve, link, Y[:, :], X[:, :], tools, 1)

        with Phase("tables3") as ph:
            stage = ph.sb("stage", [P, WG, D])
            XT = ph.sb("XT", [D, WG * P])
            TAB = ph.sb("TAB", [P, WG, R, T3])
            full = ph.sb("full", [P, WG, Q3])
            rest = ph.sb("rest", [P, WG, Q3])
            staged = ph.sem("staged")
            turned, xt_ready, p_made = ph.sem("turned"), ph.sem("xt_ready"), ph.sem("p_made")
            p_taken, q_made, tab_ready, stored = ph.sem("p_taken"), ph.sem("q_made"), ph.sem("tab_ready"), ph.sem("stored")
            gseq = ph.sem("gseq")
            wide = PS[:, BANK:8 * BANK].rearrange("p (j c) -> p j c", c=BANK)[:, :, 0:Q3]
            with nc.Block() as block:
                @block.sync
                def _(sp):
                    with sp.Fori(0, NG) as g:
                        sp.wait_ge(tab_ready, g * 4 + 4)
                        for r in range(R):
                            sp.dma_start(gate_table[bass.ds(g * (WG * P) + r * NP, WG * P), :]
                                         .rearrange("(j p) f -> p j f", p=P), TAB[:, :, r, :]).then_inc(stored, 16)
                    sp.wait_ge(stored, 16 * R * NG)

                @block.scalar
                def _(act):
                    def group(g):
                        nc.scalar.copy(stage[:, :, :], X3[:, bass.ds(g * WG, WG), :]).then_inc(staged, 1)
                        act.wait_ge(turned, g + 1)
                        if not isinstance(g, int):
                            act.wait_ge(stored, g * (16 * R))
                        nc.scalar.copy(XT[:, :], PS[0:D, 0:WG * P]).then_inc(xt_ready, 1)
                        for r in range(R):
                            nc.scalar.copy(TAB[:, :, r, 0:D], X3[:, bass.ds(g * WG, WG), :])
                        act.wait_ge(q_made, g + 1)
                        for r in range(R):
                            nc.scalar.copy(TAB[:, :, r, D:2 * D], wide[:, :, 0:D])
                            nc.scalar.copy(TAB[:, :, r, 2 * D:T3], wide[:, :, (r + 1) * D:(r + 2) * D]) \
                                .then_inc(tab_ready, 1)
                    group(0)
                    with act.Fori(1, NG) as g:
                        group(g)

                @block.vector
                def _(dve):
                    with dve.Fori(0, NG) as g:
                        gl = Chain(dve, gseq, g * 5)
                        w = bass.ds(g * WG, WG)
                        dve.wait_ge(p_made, g + 1)
                        nc.vector.tensor_tensor(full[:, :, 0:D], wide[:, :, 0:D], rows_of(vec(V_WA_B), WG), ALU.add)
                        nc.vector.tensor_copy(full[:, :, D:Q3], wide[:, :, D:Q3]).then_inc(p_taken, 1)
                        dve.wait_ge(p_taken, g + 1)
                        split3(gl, full[:, :, :], part3[:, w, 0, :], part3[:, w, 1, :], part3[:, w, 2, :],
                               rest[:, :, :])

                @block.tensor
                def _(pe):
                    def group(g):
                        if not isinstance(g, int):
                            hold(pe, "tensor", tab_ready, g * R)
                        hold(pe, "tensor", staged, g + 1)
                        for j in range(WG):
                            ins = nc.tensor.transpose(PS[0:D, j * P:(j + 1) * P], stage[:, j, :], ident[:, :])
                        ins.then_inc(turned, 1)
                        pe.wait_ge(xt_ready, g + 1)
                        for j in range(WG):
                            ins = nc.tensor.matmul(wide[:, j, :], XT[:, j * P:(j + 1) * P],
                                                   Wt[:, W_DST3:W_DST3 + Q3], start=True, stop=True)
                        ins.then_inc(p_made, 1)
                        pe.wait_ge(p_taken, g + 1)
                        for j in range(WG):
                            ins = nc.tensor.matmul(wide[:, j, :], XT[:, j * P:(j + 1) * P],
                                                   Wt[:, W_SRC3:W_SRC3 + Q3], start=True, stop=True)
                        ins.then_inc(q_made, 1)
                    group(0)
                    with pe.Fori(1, NG) as g:
                        group(g)

        with Phase("gate_a") as ph:
            G = ph.sb("G", [P, 2, B, T3])
            CODES = ph.sb("CODES", [P, 2, BE], F16)
            OHT = ph.sb("OHT", [P, 2, R, BE], BF16)
            Z = ph.sb("Z", [P, 2, B, 2 * D])
            L = ph.sb("L", [P, 2, B, D])
            HS = ph.sb("HS", [P, 2, B, AGG])
            keys_in = [ph.sem(f"keys_in{s}") for s in range(2)]
            rows_in = [ph.sem(f"rows_in{s}") for s in range(2)]
            stored = [ph.sem(f"stored{s}") for s in range(2)]
            idx_ready, oht_ready, dst_done = ph.sem("idx_ready"), ph.sem("oht_ready"), ph.sem("dst_done")
            z_ready, gate_ready, h_ready = ph.sem("z_ready"), ph.sem("gate_ready"), ph.sem("h_ready")
            seq, ones_in = ph.sem("seq"), ph.sem("ones_in")
            with nc.Block() as block:
                @block.gpsimd
                def _(pool):
                    gather_rows(pool, gate_table, lambda s, u: G[:, s, u, :], idx_ready, h_ready, rows_in)

                @block.sync
                def _(sp):
                    for s in range(2):
                        load_keys(sp, code_flat, CODES, s, s, oht_ready, keys_in)

                    def turn(t):
                        for s in range(2):
                            b = t * 2 + s
                            load_keys(sp, code_flat, CODES, b + 2, s, oht_ready, keys_in)
                            sp.wait_ge(h_ready, b + 1)
                            sp.dma_start(held[bass.ds(b * P, P), :],
                                         HS[:, s].rearrange("p b d -> p (b d)")).then_inc(stored[s], 16)
                    over_turns(sp, turn)
                    for s in range(2):
                        sp.wait_ge(stored[s], 16 * TURNS)
                        sp.wait_ge(keys_in[s], 16 * (TURNS + 1))

                @block.scalar
                def _(act):
                    def turn(t):
                        for s in range(2):
                            b = t * 2 + s
                            act.wait_ge(z_ready, b + 1)
                            nc.scalar.activation(Z[:, s, :, D:2 * D], Z[:, s, :, D:2 * D],
                                                 ACT.Sigmoid).then_inc(gate_ready, 1)
                    over_turns(act, turn)

                @block.vector
                def _(dve):
                    put_indices(row_idx, 0, 0, idx_ready)
                    put_indices(row_idx, 1, 1, idx_ready)
                    nc.vector.memset(HS[:, :, :, D:AGG], 1.0).then_inc(ones_in, 1)
                    dve.wait_ge(ones_in, 1)

                    def one_hot_nodes(s):
                        for r in range(R):
                            ins = nc.vector.tensor_scalar(OHT[:, s, r, :], CODES[:, s, :], iotaT[:, r:r + 1],
                                                          None, ALU.is_equal)
                        ins.then_inc(oht_ready, 1)

                    dve.wait_ge(keys_in[0], 16)
                    one_hot_nodes(0)

                    def turn(t):
                        for s in range(2):
                            b = t * 2 + s
                            link = Chain(dve, seq, b * 3)
                            if not (isinstance(b, int) and b == 0):
                                dve.wait_ge(dst_done, b)
                            dve.wait_ge(keys_in[1 - s], 16 * (t + 1 + s))
                            one_hot_nodes(1 - s)
                            dve.wait_ge(rows_in[s], P * (t + 1))
                            put_indices(row_idx, b + 2, s, idx_ready)
                            dve.wait_ge(dst_done, b + 1)
                            nc.vector.tensor_tensor(Z[:, s], bank(2 * s, 2).rearrange("p (b f) -> p b f", f=2 * D),
                                                    G[:, s, :, D:T3], ALU.add).then_inc(z_ready, 1)
                            dve.wait_ge(z_ready, b + 1)
                            za = Z[:, s, :, 0:D]
                            link(nc.vector.scalar_tensor_tensor(L[:, s], za, 0.01, za, ALU.mult, ALU.max))
                            link(nc.vector.tensor_tensor(L[:, s], L[:, s], rows_of(vec(V_A3), B), ALU.mult))
                            link(nc.vector.reduce_sum(score[:, bass.ds(b * B, B)], L[:, s], AX_X))
                            dve.wait_ge(gate_ready, b + 1)
                            if not (isinstance(b, int) and b < 2):
                                dve.wait_ge(stored[s], 16 * t)
                            nc.vector.tensor_tensor(HS[:, s, :, 0:D], Z[:, s, :, D:2 * D], G[:, s, :, 0:D],
                                                    ALU.mult).then_inc(h_ready, 1)
                    over_turns(dve, turn)

                @block.tensor
                def _(pe):
                    def turn(t):
                        for s in range(2):
                            b = t * 2 + s
                            at = load_places(pe, w_row, b, WINDOWS - 1)
                            pe.wait_ge(oht_ready, b + 1)
                            ring_free(pe, z_ready, b)
                            for u in range(B):
                                to = bank(2 * s + u // 4)[:, u % 4 * 2 * D:(u % 4 + 1) * 2 * D]
                                for c in range(3):
                                    mine = parts[:, bass.ds(at[u] * (3 * Q3) + c * Q3, Q3)] \
                                        .rearrange("p (k d) -> p k d", d=D)
                                    for r in range(R):
                                        ins = nc.tensor.matmul(
                                            to.rearrange("p (k d) -> p k d", d=D), OHT[:, s, r, u * P:(u + 1) * P],
                                            mine[:, 0:r + 2:r + 1, :], start=(c == 0 and r == 0),
                                            stop=(c == 2 and r == R - 1))
                            ins.then_inc(dst_done, 1)
                    over_turns(pe, turn)

        with Phase("softmax") as ph:
            SR = ph.sb("SR", [P, GROUPS, P])
            S = ph.sb("S", [P, KP])
            K = ph.sb("K", [P, KP])
            K16 = ph.sb("K16", [P, KP], BF16)
            gap = ph.sb("gap", [P, KP + 1])
            fwd = ph.sb("fwd", [P, KP])
            bwd = ph.sb("bwd", [P, KP])
            cols = ph.sb("cols", [P, 8])
            rows = ph.sb("rows", [1, 12, P])
            seq, turned, sr_ready, stored = ph.sem("seq"), ph.sem("turned"), ph.sem("sr_ready"), ph.sem("stored")
            loaded, cols_ready, rows_made = ph.sem("loaded"), ph.sem("cols_ready"), ph.sem("rows_made")
            carry_ready, carry_made, diff_ready = ph.sem("carry_ready"), ph.sem("carry_made"), ph.sem("diff_ready")
            exp_ready, stored2, loaded2, back = ph.sem("exp_ready"), ph.sem("stored2"), ph.sem("loaded2"), ph.sem("back")
            with nc.Block() as block:
                @block.sync
                def _(sp):
                    sp.dma_start(K16[:, :], key_flat.rearrange("(p j) e -> p (j e)", p=P)).then_inc(loaded, 16)
                    sp.wait_ge(sr_ready, 1)
                    sp.dma_start(score_flat.rearrange("(g p) e -> p g e", p=P), SR[:, :, :]).then_inc(stored, 16)
                    sp.wait_ge(stored, 16)
                    sp.dma_start(S[:, :], score_flat.rearrange("(p j) e -> p (j e)", p=P)).then_inc(loaded, 16)
                    sp.wait_ge(exp_ready, 1)
                    sp.dma_start(weight_flat.rearrange("(p j) e -> p (j e)", p=P), S[:, :]).then_inc(stored2, 16)
                    sp.wait_ge(stored2, 16)
                    sp.dma_start(SR[:, :, :], weight_flat.rearrange("(g p) e -> p g e", p=P)).then_inc(loaded2, 16)
                    sp.wait_ge(loaded2, 16)

                @block.scalar
                def _(act):
                    act.wait_ge(turned, 1)
                    nc.scalar.copy(SR[:, :, :].rearrange("p g e -> p (g e)"), PS[:, 0:KP]).then_inc(sr_ready, 1)
                    act.wait_ge(diff_ready, 1)
                    nc.scalar.activation(S[:, :], S[:, :], ACT.Exp).then_inc(exp_ready, 1)
                    act.wait_ge(back, 1)
                    nc.scalar.copy(score[:, :], PS[:, 0:KP])

                @block.tensor
                def _(pe):
                    for g in range(GROUPS):
                        ins = nc.tensor.transpose(PS[:, g * P:(g + 1) * P], score[:, g * P:(g + 1) * P], ident[:, :])
                    ins.then_inc(turned, 1)
                    pe.wait_ge(cols_ready, 1)
                    for c in range(5):
                        ins = nc.tensor.matmul(bank(4 + c // 4)[0:1, c % 4 * P:(c % 4 + 1) * P], cols[:, c:c + 1],
                                               ident[:, :], start=True, stop=True)
                    ins.then_inc(rows_made, 1)
                    pe.wait_ge(carry_ready, 1)
                    for c in range(2):
                        ins = nc.tensor.matmul(bank(6)[:, c:c + 1], rows[:, 10 + c, :], ident[0:1, 0:1],
                                               start=True, stop=True)
                    ins.then_inc(carry_made, 1)
                    pe.wait_ge(loaded2, 16)
                    for g in range(GROUPS):
                        ins = nc.tensor.transpose(PS[:, g * P:(g + 1) * P], SR[:, g, :], ident[:, :])
                    ins.then_inc(back, 1)

                @block.vector
                def _(dve):
                    link = Chain(dve, seq)
                    KN = KP
                    dve.wait_ge(loaded, 32)
                    link(nc.vector.tensor_copy(K[:, :], K16[:, :]))
                    link(nc.vector.memset(gap[:, :], 0.0))
                    link(nc.vector.tensor_tensor(gap[:, 1:KN], K[:, 1:KN], K[:, 0:KN - 1], ALU.not_equal))
                    link(nc.vector.tensor_scalar(gap[:, :], gap[:, :], BIG_NEG, None, ALU.mult))
                    def scan_left(initial):
                        return nc.vector.tensor_tensor_scan(fwd[:, :], gap[:, 0:KN], S[:, :], initial,
                                                            ALU.add, ALU.max)
                    def scan_right(initial):
                        return nc.vector.tensor_tensor_scan(bwd[:, ::-1], gap[:, KN:0:-1], S[:, ::-1], initial,
                                                            ALU.add, ALU.max)
                    link(scan_left(BIG_NEG))
                    link(scan_right(BIG_NEG))
                    link(nc.vector.tensor_copy(cols[:, 0:1], K[:, 0:1]))
                    link(nc.vector.tensor_copy(cols[:, 1:2], K[:, KN - 1:KN]))
                    link(nc.vector.tensor_copy(cols[:, 2:3], fwd[:, KN - 1:KN]))
                    link(nc.vector.tensor_copy(cols[:, 3:4], bwd[:, 0:1]))
                    link(nc.vector.tensor_reduce(cols[:, 4:5], gap[:, 0:KN], AX_X, ALU.min))
                    nc.vector.tensor_copy(cols[:, 5:6], cols[:, 4:5]).then_inc(cols_ready, 1)
                    dve.wait_ge(rows_made, 1)
                    for c in range(5):
                        ins = nc.vector.tensor_copy(rows[:, c, :], bank(4 + c // 4)[0:1, c % 4 * P:(c % 4 + 1) * P])
                    link(ins)
                    first, final, left, right, inner = (rows[:, c, :] for c in range(5))
                    edge, sl, sr, tl, tr = (rows[:, c, :] for c in range(5, 10))
                    into_l, into_r = rows[:, 10, :], rows[:, 11, :]
                    link(nc.vector.memset(rows[:, 5:12, :], BIG_NEG))
                    link(nc.vector.tensor_tensor(edge[:, 1:P], first[:, 1:P], final[:, 0:P - 1], ALU.not_equal))
                    link(nc.vector.tensor_scalar(edge[:, 1:P], edge[:, 1:P], BIG_NEG, None, ALU.mult))
                    link(nc.vector.tensor_tensor(tl, edge, inner, ALU.add))
                    link(nc.vector.tensor_tensor_scan(sl, tl, left, BIG_NEG, ALU.add, ALU.max))
                    link(nc.vector.tensor_tensor(into_l[:, 1:P], sl[:, 0:P - 1], edge[:, 1:P], ALU.add))
                    link(nc.vector.tensor_tensor(tr[:, 0:P - 1], edge[:, 1:P], inner[:, 0:P - 1], ALU.add))
                    link(nc.vector.tensor_tensor_scan(sr[:, ::-1], tr[:, ::-1], right[:, ::-1], BIG_NEG,
                                                      ALU.add, ALU.max))
                    nc.vector.tensor_tensor(into_r[:, 0:P - 1], sr[:, 1:P], edge[:, 1:P],
                                            ALU.add).then_inc(carry_ready, 1)
                    dve.wait_ge(carry_made, 1)
                    link(nc.vector.tensor_copy(cols[:, 6:8], bank(6)[:, 0:2]))
                    link(scan_left(cols[:, 6:7]))
                    link(scan_right(cols[:, 7:8]))
                    link(nc.vector.tensor_tensor(fwd[:, :], fwd[:, :], bwd[:, :], ALU.max))
                    nc.vector.tensor_tensor(S[:, :], S[:, :], fwd[:, :], ALU.subtract).then_inc(diff_ready, 1)

        with Phase("gate_b") as ph:
            HS = ph.sb("HS", [P, 4, B, AGG])
            T = ph.sb("T", [P, 4, B, AGG])
            MSG = ph.sb("MSG", [P, 4, 3, B, AGG], BF16)
            OH = ph.sb("OH", [P, 4, B, P], BF16)
            held_in = [ph.sem(f"held_in{s}") for s in range(4)]
            oh_ready, weighed, zeroed = ph.sem("oh_ready"), ph.sem("weighed"), ph.sem("zeroed")
            hi_ready, rest_ready, mid_ready = ph.sem("hi_ready"), ph.sem("rest_ready"), ph.sem("mid_ready")
            msg_ready, agg_done = ph.sem("msg_ready"), ph.sem("agg_done")
            with nc.Block() as block:
                @block.sync
                def _(sp):
                    def load(b, s, n):
                        ring_free4(sp, weighed, b)
                        sp.dma_start(HS[:, s].rearrange("p b d -> p (b d)"),
                                     held[bass.ds(b * P, P), :]).then_inc(held_in[s], 16)
                    over_quads(sp, load)

                @block.gpsimd
                def _(pool):
                    lower_parts(pool, T, MSG, hi_ready, rest_ready, mid_ready, msg_ready)

                @block.scalar
                def _(act):
                    def mid(b, s):
                        act.wait_ge(rest_ready, b + 1)
                        nc.scalar.copy(MSG[:, s, 1], T[:, s]).then_inc(mid_ready, 1)

                    def part(b, s, n):
                        act.wait_ge(weighed, b + 1)
                        ring_free4(act, agg_done, b)
                        nc.scalar.copy(MSG[:, s, 0], T[:, s]).then_inc(hi_ready, 1)
                        if not (isinstance(b, int) and b == 0):
                            mid(b - 1, (s - 1) % 4)
                    over_quads(act, part)
                    mid(BATCHES - 1, (BATCHES - 1) % 4)

                @block.vector
                def _(dve):
                    nc.vector.memset(PS[:, 0:NG * BANK], 0.0).then_inc(zeroed, 1)

                    def weigh(b, s, n):
                        dve.wait_ge(held_in[s], 16 * (n + 1))
                        ring_free4(dve, msg_ready, b)
                        nc.vector.tensor_tensor(
                            T[:, s], HS[:, s],
                            score[:, bass.ds(b * B, B)].unsqueeze(2).to_broadcast([P, B, AGG]),
                            ALU.mult).then_inc(weighed, 1)
                        ring_free4(dve, agg_done, b)
                        one_hot_edges(OH, s, b).then_inc(oh_ready, 1)
                    over_quads(dve, weigh)

                @block.tensor
                def _(pe):
                    pe.wait_ge(zeroed, 1)

                    def add(b, s, n):
                        at = load_places(pe, a_row, b, A_MAX)
                        pe.wait_ge(oh_ready, b + 1)
                        pe.wait_ge(msg_ready, b + 1)
                        for u in range(B):
                            for c in range(3):
                                ins = add_up(pe, OH, s, u, at[u], MSG[:, s, c, u, :], AGG)
                        ins.then_inc(agg_done, 1)
                    over_quads(pe, add)

        with Phase("node4") as ph:
            Y = ph.sb("Y", [P, WINDOWS * D])
            Y3 = Y[:, :].rearrange("p (w d) -> p w d", d=D)
            inv = ph.sb("inv", [P, WINDOWS])
            cat = parts[:, 0:WINDOWS * 4 * D].bitcast(F32).rearrange("p (w f) -> p w f", f=2 * D)
            stage = ph.sb("stage", [P, WG, 2 * D])
            XT = ph.sb("XT", [P, WG * P])
            tools = norm_tools(ph)
            seq, staged, turned, xt_ready = ph.sem("seq"), ph.sem("staged"), ph.sem("turned"), ph.sem("xt_ready")
            made, gseq, x_ready, stored = ph.sem("made"), ph.sem("gseq"), ph.sem("x_ready"), ph.sem("stored")
            with nc.Block() as block:
                @block.sync
                def _(sp):
                    sp.wait_ge(x_ready, 1)
                    full = N // P
                    sp.dma_start(out[0:full * P, :].rearrange("(w p) d -> p w d", p=P),
                                 Y3[:, 0:full, :]).then_inc(stored, 16)
                    sp.dma_start(out[full * P:N, :], Y3[0:N - full * P, full, :]).then_inc(stored, 16)
                    sp.wait_ge(stored, 32)

                @block.scalar
                def _(act):
                    with act.Fori(0, NG) as g:
                        act.wait_ge(turned, g + 1)
                        nc.scalar.copy(XT[:, :], PS[:, 0:WG * P]).then_inc(xt_ready, 1)
                    take_root(act, tools, 1)

                @block.vector
                def _(dve):
                    link = Chain(dve, seq)
                    link(nc.vector.tensor_copy(inv[:, :].rearrange("p (k j) -> p k j", j=WG), sums_psum[:, :, :, D]))
                    link(nc.vector.tensor_scalar(inv[:, :], inv[:, :], 0.5, None, ALU.max))
                    link(nc.vector.reciprocal(inv[:, :], inv[:, :]))
                    for k in range(NG):
                        nc.vector.tensor_tensor(
                            cat[:, k * WG:(k + 1) * WG, D:2 * D], sums_psum[:, k, :, 0:D],
                            inv[:, k * WG:(k + 1) * WG].unsqueeze(2).to_broadcast([P, WG, D]), ALU.mult)
                    link(nc.vector.tensor_copy(cat[:, :, 0:D], X3))
                    with dve.Fori(0, NG) as g:
                        w = bass.ds(g * WG, WG)
                        nc.vector.tensor_copy(stage[:, :, :], cat[:, w, :]).then_inc(staged, 1)
                        dve.wait_ge(made, g + 1)
                        nc.vector.tensor_tensor(Y3[:, w, :], bank(2)[:, 0:WG * D].rearrange("p (j d) -> p j d", d=D),
                                                rows_of(vec(V_LIN3_B), WG), ALU.add).then_inc(gseq, 1)
                    dve.wait_ge(gseq, NG)
                    link(nc.vector.scalar_tensor_tensor(Y[:, :], Y[:, :], 0.01, Y[:, :], ALU.mult, ALU.max))
                    link(nc.vector.tensor_tensor(Y[:, :], Y[:, :], X[:, :], ALU.add))
                    layer_norm(dve, link, Y[:, :], Y[:, :], tools, 1)
                    nc.vector.tensor_copy(X[:, 0:1], Y[:, 0:1]).then_inc(x_ready, 1)

                @block.tensor
                def _(pe):
                    with pe.Fori(0, NG) as g:
                        hold(pe, "tensor", staged, g + 1)
                        for j in range(WG):
                            ins = nc.tensor.transpose(PS[:, j * P:(j + 1) * P], stage[:, j, :], ident[:, :])
                        ins.then_inc(turned, 1)
                        pe.wait_ge(xt_ready, g + 1)
                        for j in range(WG):
                            ins = nc.tensor.matmul(bank(2)[:, j * D:(j + 1) * D], XT[:, j * P:(j + 1) * P], L3[:, :],
                                                   start=True, stop=True)
                        ins.then_inc(made, 1)


def kernel(x, src, dst, edge_type_4, L1_gnn_lin_w, L1_gnn_attn_src, L1_gnn_attn_dst, L1_gnn_out_w, L1_gnn_out_b,
           L1_gnn_ln_g, L1_gnn_ln_b, L2_gnn_W, L2_gnn_b, L2_gnn_gamma, L2_gnn_beta, L3_gnn_r, L3_gnn_a,
           L3_gnn_Wa_w, L3_gnn_Wa_b, L3_gnn_lin_w, L3_gnn_lin_b):
    import concourse.bacc as bacc
    from concourse.bass_utils import run_bass_kernel_spmd

    def tiles(a, pad):
        a = np.asarray(a)
        return np.concatenate([a, np.full(KP * P - E, pad, a.dtype)]).reshape(KP, P)

    edges = np.concatenate([tiles(src, 0), tiles(dst, FAR), tiles(edge_type_4, 0)], axis=1)
    x_pad = np.concatenate([np.asarray(x), np.zeros((NP - N, D), np.float32)])
    lin_w = np.asarray(L1_gnn_lin_w).reshape(H, D, D).transpose(1, 0, 2).reshape(D, H * D)
    out_w = np.asarray(L1_gnn_out_w).reshape(D, H, D).transpose(2, 1, 0).reshape(D, H * D)
    r3 = np.asarray(L3_gnn_r).transpose(1, 0, 2).reshape(2 * D, R * D)
    wa = np.asarray(L3_gnn_Wa_w).T
    edge_w = np.asarray(L2_gnn_W).T
    weights = np.concatenate([
        lin_w, out_w, np.asarray(L1_gnn_attn_src).T, np.asarray(L1_gnn_attn_dst).T,
        edge_w[:D], edge_w[D:], wa[:D], r3[:D], wa[D:], r3[D:]], axis=1)
    vectors = np.concatenate([np.asarray(v).reshape(-1) for v in (
        L1_gnn_out_b, L1_gnn_ln_g, L1_gnn_ln_b, L2_gnn_b, L2_gnn_gamma, L2_gnn_beta,
        np.asarray(L3_gnn_a)[0], L3_gnn_Wa_b, L3_gnn_lin_b)]).reshape(1, NVEC * D)
    order_src = tiles(src, NP)
    arrays = {"x_pad": x_pad, "edges": edges, "order_src": order_src, "weights": weights, "vectors": vectors,
              "lin3": np.asarray(L3_gnn_lin_w).T}
    arrays = {n: np.ascontiguousarray(a) for n, a in arrays.items()}

    nc = bacc.Bacc("TRN2", target_bir_lowering=False, num_devices=1)
    args = [nc.dram_tensor(n, a.shape, mybir.dt.from_np(a.dtype), kind="ExternalInput").ap()
            for n, a in arrays.items()]
    out = nc.dram_tensor("out", (N, D), F32, kind="ExternalOutput").ap()
    build(nc, *args, out)
    result = run_bass_kernel_spmd(nc, [arrays], core_ids=[0])
    return result.results[0]["out"]
```
